# Optimizing a Trainium2 kernel written in Bass

```python
import numpy as np
import jax
import jax.numpy as jnp

def _softmax(x, axis=-1):
    return jax.nn.softmax(x, axis=axis)

def _gelu(x):
    return jax.nn.gelu(x, approximate=True)

def _silu(x):
    return jax.nn.silu(x)

def _sigmoid(x):
    return jax.nn.sigmoid(x)

def _layernorm(x, axis=-1, eps=1e-05):
    m = jnp.mean(x, axis=axis, keepdims=True)
    v = jnp.var(x, axis=axis, keepdims=True)
    return (x - m) / jnp.sqrt(v + eps)

def _scatter_add(tgt, idx, src, axis=0):
    return tgt.at[idx].add(src)

def _segment_sum(src, seg, n):
    return jax.ops.segment_sum(src, seg, n)
kernel_name = 'mk_gnn_resnorm_d4_gnn_r64_986ae4'

def setup_inputs(seed: int=0):
    np.random.seed(seed)
    _w = jnp.asarray

    def _rec_inputs():
        import jax
        import jax.numpy as jnp
        _gk = jax.random.key(seed)
        x = -0.0005121 + 1.001 * jax.random.normal(jax.random.fold_in(_gk, 1), (100000, 64), jnp.float32)
        src = jax.random.randint(jax.random.fold_in(_gk, 2), (50000,), 0, 100000, jnp.int32)
        dst = jnp.minimum((100000 * jax.random.uniform(jax.random.fold_in(_gk, 3), (50000,)) ** 2.0).astype(jnp.int32), 99999)
        _o = jnp.argsort(dst, stable=True)
        src = src[_o]
        dst = dst[_o]
        edge_attr_8 = -0.000153872 + 1.00011 * jax.random.normal(jax.random.fold_in(_gk, 12), (50000, 8), jnp.float32)
        edge_type_8 = jax.random.randint(jax.random.fold_in(_gk, 13), (50000,), 0, 8, jnp.int32)
        edge_weight = 0.000937891 + 0.999965 * jax.random.normal(jax.random.fold_in(_gk, 14), (50000,), jnp.float32)
        return (x, src, dst, edge_attr_8, edge_type_8, edge_weight)
    x, src, dst, edge_attr_8, edge_type_8, edge_weight = _rec_inputs()

    def _L0_gnn_setup():
        import jax, jax.numpy as jnp
        import numpy as np
        N_NODES = 50000
        N_EDGES = 12500
        D_IN = 64
        D_H0 = 64
        D_H1 = 64
        N_RELS = 8
        N_BASES = 4

        def _rel_graph_conv(h, src, dst, etype, basis, coeff, loop_w, bias):
            W = jnp.einsum('rb,bio->rio', coeff, basis)
            XW = jnp.einsum('ni,rio->rno', h, W)
            m = XW[etype, src]
            agg = jax.ops.segment_sum(m, dst, num_segments=h.shape[0])
            return agg + h @ loop_w + bias
        key = jax.random.key(seed)
        ks = jax.random.split(key, 12)
        return {'x': jax.random.normal(ks[0], (N_NODES, D_IN), dtype=jnp.float32), 'src': jax.random.randint(ks[1], (N_EDGES,), 0, N_NODES, dtype=jnp.int64), 'dst': jax.random.randint(ks[2], (N_EDGES,), 0, N_NODES, dtype=jnp.int64), 'etype': jax.random.randint(ks[3], (N_EDGES,), 0, N_RELS, dtype=jnp.int64), 'basis1': jax.random.normal(ks[4], (N_BASES, D_IN, D_H0), dtype=jnp.float32) * 0.05, 'coeff1': jax.random.normal(ks[5], (N_RELS, N_BASES), dtype=jnp.float32), 'loop_w1': jax.random.normal(ks[6], (D_IN, D_H0), dtype=jnp.float32) * 0.05, 'bias1': jnp.zeros((D_H0,), dtype=jnp.float32), 'basis2': jax.random.normal(ks[7], (N_BASES, D_H0, D_H1), dtype=jnp.float32) * 0.05, 'coeff2': jax.random.normal(ks[8], (N_RELS, N_BASES), dtype=jnp.float32), 'loop_w2': jax.random.normal(ks[9], (D_H0, D_H1), dtype=jnp.float32) * 0.05, 'bias2': jnp.zeros((D_H1,), dtype=jnp.float32)}
    _L0_gnn_all = _L0_gnn_setup()
    _L0_gnn_in = {k: v for k, v in _L0_gnn_all.items() if k in ('basis1', 'coeff1', 'loop_w1', 'bias1', 'basis2', 'coeff2', 'loop_w2', 'bias2')}
    del _L0_gnn_all

    def _L1_gnn_setup():
        import jax, jax.numpy as jnp
        import numpy as np
        N_NODES = 20000
        N_EDGES = 15625
        C = 64
        H = 64
        N_BASIS = 8
        key = jax.random.key(seed)
        ks = jax.random.split(key, 10)

        def glorot(k, shape):
            fan_in, fan_out = (shape[0], shape[1])
            lim = np.sqrt(6.0 / (fan_in + fan_out)).astype(np.float32)
            return jax.random.uniform(k, shape, jnp.float32, -lim, lim)
        return {'p': jax.random.normal(ks[0], (N_NODES, C), jnp.float32), 'idx_i': jax.random.randint(ks[1], (N_EDGES,), 0, N_NODES), 'idx_j': jax.random.randint(ks[2], (N_EDGES,), 0, N_NODES), 'basis': jax.random.normal(ks[3], (N_EDGES, N_BASIS), jnp.float32), 'pp_W': glorot(ks[4], (C, C)), 'pp_b': jnp.zeros((C,), jnp.float32), 'pi_W1': glorot(ks[5], (2 * C, H)), 'pi_b1': jnp.zeros((H,), jnp.float32), 'pi_W2': glorot(ks[6], (H, H * N_BASIS)), 'ii_W': glorot(ks[7], (H, C)), 'ii_b': jnp.zeros((C,), jnp.float32)}
    _L1_gnn_all = _L1_gnn_setup()
    _L1_gnn_in = {k: v for k, v in _L1_gnn_all.items() if k in ('pp_W', 'pp_b', 'pi_W1', 'pi_b1', 'pi_W2', 'ii_W', 'ii_b')}
    del _L1_gnn_all

    def _L2_gnn_setup():
        import jax, jax.numpy as jnp
        import numpy as np
        N_NODES = 50000
        N_EDGES = 12500
        D = 64

        def _gnn_layer(nf, traj, src, dst, We, be, Wn, bn):
            ef = jnp.concatenate([nf[src], nf[dst], traj[:, None]], axis=-1)
            msg = jax.nn.leaky_relu(ef @ We.T + be, negative_slope=0.01)
            red = jax.ops.segment_sum(msg, dst, num_segments=nf.shape[0])
            h = jnp.concatenate([nf, red], axis=-1)
            return jax.nn.leaky_relu(h @ Wn.T + bn, negative_slope=0.01)
        key = jax.random.key(seed)
        ks = jax.random.split(key, 20)
        inp = {'nf': jax.random.normal(ks[0], (N_NODES, D), dtype=jnp.float32), 'traj': jax.random.normal(ks[1], (N_EDGES,), dtype=jnp.float32), 'src': jax.random.randint(ks[2], (N_EDGES,), 0, N_NODES), 'dst': jax.random.randint(ks[3], (N_EDGES,), 0, N_NODES)}
        s = 0.05
        for l in range(3):
            inp[f'We{l}'] = jax.random.normal(ks[4 + 4 * l], (D, 2 * D + 1), dtype=jnp.float32) * s
            inp[f'be{l}'] = jax.random.normal(ks[5 + 4 * l], (D,), dtype=jnp.float32) * s
            inp[f'Wn{l}'] = jax.random.normal(ks[6 + 4 * l], (D, 2 * D), dtype=jnp.float32) * s
            inp[f'bn{l}'] = jax.random.normal(ks[7 + 4 * l], (D,), dtype=jnp.float32) * s
        return inp
    _L2_gnn_all = _L2_gnn_setup()
    _L2_gnn_in = {k: v for k, v in _L2_gnn_all.items() if k in ('We0', 'be0', 'Wn0', 'bn0', 'We1', 'be1', 'Wn1', 'bn1', 'We2', 'be2', 'Wn2', 'bn2')}
    del _L2_gnn_all

    def _L3_gnn_setup():
        import jax, jax.numpy as jnp
        import numpy as np
        N_NODES = 100000
        N_EDGES = 50000
        N_RELS = 8
        F_IN = 64
        F_OUT = 64
        key = jax.random.key(seed)
        k1, k2, k3, k4, k5, k6 = jax.random.split(key, 6)
        X = jax.random.normal(k1, (N_NODES, F_IN), dtype=jnp.float32)
        W = jax.random.normal(k2, (N_RELS, F_IN, F_OUT), dtype=jnp.float32) * 0.1
        A = jax.random.uniform(k3, (N_EDGES,), dtype=jnp.float32)
        src = jax.random.randint(k4, (N_EDGES,), 0, N_NODES, dtype=jnp.int32)
        dst = jax.random.randint(k5, (N_EDGES,), 0, N_NODES, dtype=jnp.int32)
        etype = jax.random.randint(k6, (N_EDGES,), 0, N_RELS, dtype=jnp.int32)
        return {'X': X, 'W': W, 'A': A, 'src': src, 'dst': dst, 'etype': etype}
    _L3_gnn_all = _L3_gnn_setup()
    _L3_gnn_in = {k: v for k, v in _L3_gnn_all.items() if k in ('W',)}
    del _L3_gnn_all
    return {'x': x, 'src': src, 'dst': dst, 'edge_attr_8': edge_attr_8, 'edge_type_8': edge_type_8, 'edge_weight': edge_weight, 'L0_gnn_basis1': _L0_gnn_in['basis1'], 'L0_gnn_coeff1': _L0_gnn_in['coeff1'], 'L0_gnn_loop_w1': _L0_gnn_in['loop_w1'], 'L0_gnn_bias1': _L0_gnn_in['bias1'], 'L0_gnn_basis2': _L0_gnn_in['basis2'], 'L0_gnn_coeff2': _L0_gnn_in['coeff2'], 'L0_gnn_loop_w2': _L0_gnn_in['loop_w2'], 'L0_gnn_bias2': _L0_gnn_in['bias2'], 'L1_gnn_pp_W': _L1_gnn_in['pp_W'], 'L1_gnn_pp_b': _L1_gnn_in['pp_b'], 'L1_gnn_pi_W1': _L1_gnn_in['pi_W1'], 'L1_gnn_pi_b1': _L1_gnn_in['pi_b1'], 'L1_gnn_pi_W2': _L1_gnn_in['pi_W2'], 'L1_gnn_ii_W': _L1_gnn_in['ii_W'], 'L1_gnn_ii_b': _L1_gnn_in['ii_b'], 'L2_gnn_We0': _L2_gnn_in['We0'], 'L2_gnn_be0': _L2_gnn_in['be0'], 'L2_gnn_Wn0': _L2_gnn_in['Wn0'], 'L2_gnn_bn0': _L2_gnn_in['bn0'], 'L2_gnn_We1': _L2_gnn_in['We1'], 'L2_gnn_be1': _L2_gnn_in['be1'], 'L2_gnn_Wn1': _L2_gnn_in['Wn1'], 'L2_gnn_bn1': _L2_gnn_in['bn1'], 'L2_gnn_We2': _L2_gnn_in['We2'], 'L2_gnn_be2': _L2_gnn_in['be2'], 'L2_gnn_Wn2': _L2_gnn_in['Wn2'], 'L2_gnn_bn2': _L2_gnn_in['bn2'], 'L3_gnn_W': _L3_gnn_in['W']}

def reference(x, src, dst, edge_attr_8, edge_type_8, edge_weight, L0_gnn_basis1, L0_gnn_coeff1, L0_gnn_loop_w1, L0_gnn_bias1, L0_gnn_basis2, L0_gnn_coeff2, L0_gnn_loop_w2, L0_gnn_bias2, L1_gnn_pp_W, L1_gnn_pp_b, L1_gnn_pi_W1, L1_gnn_pi_b1, L1_gnn_pi_W2, L1_gnn_ii_W, L1_gnn_ii_b, L2_gnn_We0, L2_gnn_be0, L2_gnn_Wn0, L2_gnn_bn0, L2_gnn_We1, L2_gnn_be1, L2_gnn_Wn1, L2_gnn_bn1, L2_gnn_We2, L2_gnn_be2, L2_gnn_Wn2, L2_gnn_bn2, L3_gnn_W):
    import jax
    import jax.numpy as jnp

    def _L0_gnn_ref(x, src, dst, etype, basis1, coeff1, loop_w1, bias1, basis2, coeff2, loop_w2, bias2):
        import jax, jax.numpy as jnp
        import numpy as np
        N_NODES = 50000
        N_EDGES = 12500
        D_IN = 64
        D_H0 = 64
        D_H1 = 64
        N_RELS = 8
        N_BASES = 4

        def _rel_graph_conv(h, src, dst, etype, basis, coeff, loop_w, bias):
            W = jnp.einsum('rb,bio->rio', coeff, basis)
            XW = jnp.einsum('ni,rio->rno', h, W)
            m = XW[etype, src]
            agg = jax.ops.segment_sum(m, dst, num_segments=h.shape[0])
            return agg + h @ loop_w + bias
        h = _rel_graph_conv(x, src, dst, etype, basis1, coeff1, loop_w1, bias1)
        h = jax.nn.leaky_relu(h)
        h = _rel_graph_conv(h, src, dst, etype, basis2, coeff2, loop_w2, bias2)
        return h

    def _L1_gnn_ref(p, idx_i, idx_j, basis, pp_W, pp_b, pi_W1, pi_b1, pi_W2, ii_W, ii_b):
        import jax, jax.numpy as jnp
        import numpy as np
        N_NODES = 20000
        N_EDGES = 15625
        C = 64
        H = 64
        N_BASIS = 8
        p1 = jnp.tanh(p @ pp_W + pp_b)
        pair = jnp.concatenate([p1[idx_i], p1[idx_j]], axis=-1)
        h = pair @ pi_W1 + pi_b1
        h = (h @ pi_W2).reshape(-1, H, N_BASIS)
        i1 = jnp.einsum('ecb,eb->ec', h, basis)
        i2 = jnp.tanh(i1 @ ii_W + ii_b)
        return p.at[idx_i].add(i2)

    def _L2_gnn_ref(nf, traj, src, dst, We0, be0, Wn0, bn0, We1, be1, Wn1, bn1, We2, be2, Wn2, bn2):
        import jax, jax.numpy as jnp
        import numpy as np
        N_NODES = 50000
        N_EDGES = 12500
        D = 64

        def _gnn_layer(nf, traj, src, dst, We, be, Wn, bn):
            ef = jnp.concatenate([nf[src], nf[dst], traj[:, None]], axis=-1)
            msg = jax.nn.leaky_relu(ef @ We.T + be, negative_slope=0.01)
            red = jax.ops.segment_sum(msg, dst, num_segments=nf.shape[0])
            h = jnp.concatenate([nf, red], axis=-1)
            return jax.nn.leaky_relu(h @ Wn.T + bn, negative_slope=0.01)
        params = [(We0, be0, Wn0, bn0), (We1, be1, Wn1, bn1), (We2, be2, Wn2, bn2)]
        h = nf
        for We, be, Wn, bn in params:
            h = _gnn_layer(h, traj, src, dst, We, be, Wn, bn)
        return h

    def _L3_gnn_ref(X, W, A, src, dst, etype):
        import jax, jax.numpy as jnp
        import numpy as np
        N_NODES = 100000
        N_EDGES = 50000
        N_RELS = 8
        F_IN = 64
        F_OUT = 64
        XW = jnp.einsum('nf,rfo->rno', X, W)
        msg = XW[etype, src] * A[:, None]
        Y = jax.ops.segment_sum(msg, dst, num_segments=X.shape[0])
        return Y
    x = _layernorm(x + _L0_gnn_ref(x, src, dst, edge_type_8, L0_gnn_basis1, L0_gnn_coeff1, L0_gnn_loop_w1, L0_gnn_bias1, L0_gnn_basis2, L0_gnn_coeff2, L0_gnn_loop_w2, L0_gnn_bias2), axis=-1)
    x = _layernorm(x + _L1_gnn_ref(x, src, dst, edge_attr_8, L1_gnn_pp_W, L1_gnn_pp_b, L1_gnn_pi_W1, L1_gnn_pi_b1, L1_gnn_pi_W2, L1_gnn_ii_W, L1_gnn_ii_b), axis=-1)
    x = _layernorm(x + _L2_gnn_ref(x, edge_weight, src, dst, L2_gnn_We0, L2_gnn_be0, L2_gnn_Wn0, L2_gnn_bn0, L2_gnn_We1, L2_gnn_be1, L2_gnn_Wn1, L2_gnn_bn1, L2_gnn_We2, L2_gnn_be2, L2_gnn_Wn2, L2_gnn_bn2), axis=-1)
    x = _layernorm(x + _L3_gnn_ref(x, L3_gnn_W, edge_weight, src, dst, edge_type_8), axis=-1)
    return x

_drawn_inputs = setup_inputs


def setup_inputs(seed=0):
    import zlib

    import numpy as np

    out = dict(_drawn_inputs(seed))
    spreads = {'L0_gnn_bias1': (0.0, 0.1),
     'L0_gnn_bias2': (0.0, 0.1),
     'L1_gnn_pp_b': (0.0, 0.333),
     'L1_gnn_pi_b1': (0.0, 0.1),
     'L1_gnn_ii_b': (0.0, 0.1)}
    factors = {'L2_gnn_We0': 6.168,
     'L2_gnn_be0': 8.0,
     'L2_gnn_Wn0': 2.793,
     'L2_gnn_bn0': 8.0,
     'L2_gnn_We1': 4.859,
     'L2_gnn_be1': 27.195,
     'L2_gnn_bn1': 5.524,
     'L2_gnn_We2': 3.272,
     'L2_gnn_be2': 8.0}
    for name, (base, spread) in spreads.items():
        noise = np.random.default_rng([zlib.crc32(name.encode()), seed]).standard_normal(out[name].shape)
        drawn = base * np.exp(spread * noise) if base else spread * noise
        out[name] = jnp.asarray(drawn.astype(out[name].dtype))
    for name, factor in factors.items():
        out[name] = (out[name] * factor).astype(out[name].dtype)
    return out
```

```python
from contextlib import ExitStack

import concourse.bass as bass
from concourse import mybir

F32 = mybir.dt.float32
I32 = mybir.dt.int32
ALU = mybir.AluOpType
ACT = mybir.ActivationFunctionType
AX = mybir.AxisListType

P = 128
D = 64
G = 4
W = G * P
K = 16
R = 8
NB = 4
SLOTS = 4
EPS = 1e-5
SLOPE = 0.01
SEED = 4


def build(nc, a, out):
    N = a["x"].shape[0]
    E = a["src"].shape[0]
    Q = -(-E // (2 * W)) * 2
    T = Q * G
    PF, PR = E // T, E % T
    PAD = 1 << 20
    assert N < PAD and W >= P
    CH = P * K
    FULL = N // CH
    TAILP = (N - FULL * CH) // K
    assert FULL * CH + TAILP * K == N
    LOOPS = FULL // SLOTS
    CHUNKS = FULL + (TAILP > 0)
    TB = -(-T // P)

    ctx = ExitStack()
    with ctx:
        def sb(name, shape, dt=F32):
            return ctx.enter_context(nc.sbuf_tensor(name, shape, dt))[tuple(slice(None) for _ in shape)]

        def ps(name, shape):
            return ctx.enter_context(nc.psum_tensor(name, shape, F32))[:, :]

        def dram(name, rows, cols=D):
            return nc.dram_tensor(name, [rows, cols], F32, kind="Internal").ap()

        base1 = dram("base1", N + W)
        base2 = dram("base2", N + W)
        base3 = dram("base3", N + W)
        mlp1 = dram("mlp1", N + W)
        mlp2 = dram("mlp2", N + W)
        mlp3 = dram("mlp3", N + W)
        base4 = dram("base4", N + W)
        p1 = dram("p1", N)
        x2 = dram("x2", N)
        x3 = dram("x3", N)
        rows_dst = dram("rows_dst", T, P)
        rows_src = dram("rows_src", T, P)

        ident = sb("ident", [P, P])
        earlier = sb("earlier", [P, G, W])
        spare = sb("spare", [P, Q, G], I32)
        epst = sb("epst", [P, 1])
        zero = sb("zero", [P, G, D])
        loop1 = sb("loop1", [P, P])
        loop2 = sb("loop2", [P, P])
        ppw = sb("ppw", [P, P])
        wna = [sb(f"wna{l}", [P, P]) for l in range(3)]
        wnb = [sb(f"wnb{l}", [D, D]) for l in range(3)]
        we = [sb(f"we{l}", [P, D]) for l in range(3)]
        wet = [sb(f"wet{l}", [P, D]) for l in range(3)]
        bas1 = sb("bas1", [P, NB // 2, D])
        bas2 = sb("bas2", [P, NB // 2, D])
        w3 = sb("w3", [P, R // 2, D])
        piw1 = sb("piw1", [P, D])
        fold = sb("fold", [P, R // 2, D])
        names = ["L0_gnn_bias1", "L0_gnn_bias2", "L1_gnn_pp_b", "L1_gnn_pi_b1", "L1_gnn_ii_b",
                 "L2_gnn_be0", "L2_gnn_be1", "L2_gnn_be2", "L2_gnn_bn0", "L2_gnn_bn1", "L2_gnn_bn2"]
        bias = {n: sb("b_" + n, [P, D]) for n in names}
        iiw = sb("iiw", [D, D])
        piw2 = sb("piw2", [D, D * R])
        piw2b = sb("piw2b", [D, R, D])
        piw2t = sb("piw2t", [D, R, D])
        we_in = [sb(f"we_in{l}", [D, 2 * D + 1]) for l in range(3)]
        wet_in = sb("wet_in", [D, 3, P])
        wna_in = [sb(f"wna_in{l}", [D, 2, D]) for l in range(3)]
        wnb_in = [sb(f"wnb_in{l}", [D, 2, D]) for l in range(3)]
        cf1 = sb("cf1", [P, R, NB])
        cf2 = sb("cf2", [P, R, NB])

        key_in = {"dst": sb("dst_in", [P, T], I32), "src": sb("src_in", [P, T], I32)}
        typ_in = sb("typ_in", [P, T], I32)
        key = {"dst": sb("key_dst", [P, T]), "src": sb("key_src", [P, T])}
        ends = sb("ends", [P, Q, 2, G], I32)
        target = {"dst": sb("target_dst", [P, T], I32), "src": sb("target_src", [P, T], I32)}
        before = sb("before", [P, T])
        work = sb("work", [P, T])
        weight = sb("weight", [P, T])
        attr = sb("attr", [P, T, R])
        coef1 = sb("coef1", [P, T, NB])
        coef2 = sb("coef2", [P, T, NB])
        coef3 = sb("coef3", [P, T, R])
        rowblk = sb("rowblk", [P, TB, P])

        rows = [sb(f"rows{s}", [P, W]) for s in range(2)]
        gidx = [sb(f"gidx{s}", [P, 2, G], I32) for s in range(2)]
        sidx = [sb(f"sidx{s}", [P, G], I32) for s in range(2)]
        X = [sb(f"X{s}", [P, G, 2, D]) for s in range(2)]
        same = [sb(f"same{s}", [P, G, W]) for s in range(2)]
        cnt = [sb(f"cnt{s}", [P, G]) for s in range(2)]
        XT = sb("XT", [P, W])
        hid = sb("hid", [P, G, D])
        msg = sb("msg", [P, G, D])
        sumT = sb("sumT", [D, W])
        sums = [sb(f"sums{s}", [P, G, D]) for s in range(2)]
        big = [sb(f"big{s}", [P, 2 * K * D]) for s in range(2)]
        Y = big[0]
        YT = big[1]

        in1 = [sb(f"in1_{s}", [P, K, D]) for s in range(SLOTS)]
        in2 = [sb(f"in2_{s}", [P, K, D]) for s in range(SLOTS)]
        v = [sb(f"v{s}", [P, K, D]) for s in range(2)]
        vT = [big[s][:, 0:K * D] for s in range(2)]
        sq = [big[s][:, K * D:2 * K * D] for s in range(2)]
        o1 = [sb(f"o1_{s}", [P, K, D]) for s in range(SLOTS)]
        o2 = [same[s // 2][:, 2 * (s % 2):2 * (s % 2) + 2, :].rearrange("p a (b d) -> p (a b) d", d=D)
              for s in range(SLOTS)]
        stat = [sb(f"stat{s}", [P, 5, K]) for s in range(SLOTS)]

        tp = [ps(f"tp{s}", [P, 2 * W]) for s in range(2)]
        mm = [ps(f"mm{s}", [P, 2 * W]) for s in range(2)]
        ps_hid = mm[0][:, 0:G * D]
        ps_msg = mm[0][:, W:W + G * D]
        ps_sumT = mm[1][0:D, 0:W]
        ps_sum = mm[1][:, W:W + G * D]

        def node(src, prep, outs, mat=None, shift=None, src2=None, add=False, tanh=False):
            return dict(kind="node", src=src, src2=src2, prep=prep, mat=mat, shift=shift, add=add, tanh=tanh, outs=outs)

        def edge(kind, table, to, by="dst", **more):
            return dict(kind=kind, table=table, to=to, by=by, **more)

        passes = [
            node(a["x"], "none", [(base1, "o1")], loop1, "L0_gnn_bias1"),
            edge("rel", a["x"], base1, coef=coef1, mat=bas1, terms=NB, act=False),
            node(base1, "leaky", [(base2, "o1")], loop2, "L0_gnn_bias2", src2=a["x"], add=True),
            edge("rel", base1, base2, coef=coef2, mat=bas2, terms=NB, act=True),
            node(base2, "norm", [(base3, "o1"), (p1, "o2")], ppw, "L1_gnn_pp_b", tanh=True),
            edge("pair", p1, base3, by="src", coef=attr, mat=fold, terms=R, act=False),
            node(base3, "norm", [(mlp1, "o1"), (x2, "o2")], wna[0], "L2_gnn_bn0"),
            edge("mlp", x2, mlp1, layer=0, act=False),
            node(mlp1, "leaky", [(mlp2, "o1")], wna[1], "L2_gnn_bn1"),
            edge("mlp", mlp1, mlp2, layer=1, act=True),
            node(mlp2, "leaky", [(mlp3, "o1")], wna[2], "L2_gnn_bn2"),
            edge("mlp", mlp2, mlp3, layer=2, act=True),
            node(mlp3, "leaky add norm", [(x3, "o1"), (base4, "o1")], src2=x2),
            edge("rel", x3, base4, coef=coef3, mat=w3, terms=R, act=False),
            node(base4, "norm", [(out, "o1")]),
        ]

        def sem(name):
            return ctx.enter_context(nc.semaphore(name))

        class Count:

            def __init__(self, name, start):
                self.sem, self.at, self.total = sem(name), [], start

        counts = {}

        def counted(name, start=SEED):
            counts[name] = Count(name, start)
            return counts[name]

        loaded = [counted(f"loaded{s}", 0) for s in range(SLOTS)]
        stored = [counted(f"stored{s}", 0) for s in range(SLOTS)]
        rows_in = [counted(f"rows_in{s}", 0) for s in range(2)]
        gidx_in = [counted(f"gidx_in{s}", 0) for s in range(2)]
        sidx_in = [counted(f"sidx_in{s}", 0) for s in range(2)]
        gathered = [counted(f"gathered{s}", 0) for s in range(2)]
        scattered = [counted(f"scattered{s}", 0) for s in range(2)]
        per_item = ["activated", "added", "summed", "averaged", "centered", "squared", "sq_summed",
                    "rooted", "inverted", "normed", "doubled", "transposed", "moved", "multiplied", "biased",
                    "completed", "tanhed",
                    "compared", "x_used", "pair_transposed", "pair_moved", "hid_ready", "hid_biased", "expanded",
                    "exp_transposed", "exp_moved", "msg_ready", "msg_biased", "msg_moved", "edge_term",
                    "edge_biased", "hid_summed", "sumT_ready", "sumT_moved", "sum_ready", "sum_moved"]
        c = {n: counted(n) for n in per_item}
        pool_past = sem("pool_past")
        seeded = sem("seeded")

        def does_mm(q):
            return q["mat"] is not None

        for q in passes:
            for x in counts.values():
                x.at.append(x.total)
            if q["kind"] == "node":
                for s in range(SLOTS):
                    n = len([i for i in range(CHUNKS) if i % SLOTS == s])
                    loaded[s].total += 16 * n * (1 + (q["src2"] is not None))
                    stored[s].total += 16 * n * len(q["outs"])
                used = {"none": [], "leaky": ["activated"],
                        "norm": ["summed", "averaged", "centered", "squared", "sq_summed", "rooted", "inverted",
                                 "normed"],
                        "leaky add norm": ["activated", "added", "summed", "averaged", "centered", "squared",
                                           "sq_summed", "rooted", "inverted", "normed"]}[q["prep"]]
                used = used + (["transposed", "moved", "multiplied", "biased"] if does_mm(q) else [])
                used = used + (["completed"] if q["add"] else []) + (["doubled", "tanhed"] if q["tanh"] else [])
                for n in used:
                    c[n].total += CHUNKS
            else:
                ends_of = 1 if q["kind"] == "rel" else 2
                for s in range(2):
                    rows_in[s].total += 16 * (Q // 2)
                    gidx_in[s].total += 16 * (Q // 2)
                    sidx_in[s].total += 16 * (Q // 2)
                    gathered[s].total += 16 * G * ends_of * (Q // 2)
                    scattered[s].total += 16 * G * (Q // 2)
                used = ["compared", "x_used", "sum_ready", "sum_moved"] + (["activated"] if q["act"] else [])
                if q["kind"] in ("rel", "pair"):
                    used += ["expanded", "exp_transposed", "exp_moved", "msg_ready", "msg_moved"]
                if q["kind"] in ("pair", "mlp"):
                    used += ["pair_transposed", "pair_moved", "hid_ready"]
                if q["kind"] == "pair":
                    used += ["hid_biased", "msg_biased"]
                if q["kind"] == "mlp":
                    used += ["edge_term", "edge_biased", "hid_summed", "msg_moved", "sumT_ready", "sumT_moved"]
                for n in used:
                    c[n].total += Q
        spare_writes = list(zip([base1, base2, base3, mlp1, mlp2, mlp3, base4],
                                [stored[0], stored[1], stored[2], stored[3], scattered[0], scattered[1], scattered[1]]))
        for _, x in spare_writes:
            x.total += 16
            x.at = [n + 16 for n in x.at]

        def item(name, i, n):
            return c[name].at[i] + n

        def end_of_pass(counter, i):
            return counter.at[i + 1] if i + 1 < len(passes) else counter.total

        setup_in = sem("setup_in")
        cleared = sem("cleared")
        made = sem("made")
        step = sem("step")
        product = sem("product")
        rows_out = sem("rows_out")
        ranked = sem("ranked")
        rank_rows = [sem(f"rank_rows{s}") for s in range(2)]
        noted = sem("noted")

        rows_made = sem("rows_made")
        weights_in = sem("weights_in")
        turned = sem("turned")
        setup_done = sem("setup_done")
        block = ctx.enter_context(nc.Block())

        setup_loads = []

        def note(dst, src):
            setup_loads.append((dst, src))

        for t, w in ((loop1, a["L0_gnn_loop_w1"]), (loop2, a["L0_gnn_loop_w2"]), (ppw, a["L1_gnn_pp_W"])):
            note(t[0:D, 0:D], w[:, :])
            note(t[D:P, D:P], w[:, :])
        for t, w in ((bas1, a["L0_gnn_basis1"]), (bas2, a["L0_gnn_basis2"]), (w3, a["L3_gnn_W"])):
            flat = w.rearrange("r i o -> (r i) o")
            for k in range(flat.shape[0] // P):
                note(t[:, k, :], flat[k * P:(k + 1) * P, :])
        note(piw1[:, :], a["L1_gnn_pi_W1"][:, :])
        note(piw2[:, :], a["L1_gnn_pi_W2"][:, :])
        note(iiw[:, :], a["L1_gnn_ii_W"][:, :])
        for l in range(3):
            note(we_in[l][:, :], a[f"L2_gnn_We{l}"][:, :])
            for h in range(2):
                note(wna_in[l][:, h, :], a[f"L2_gnn_Wn{l}"][:, 0:D])
                note(wnb_in[l][:, h, :], a[f"L2_gnn_Wn{l}"][:, D:2 * D])
        for n in names:
            note(bias[n][:, :], a[n].partition_broadcast(P))
        note(cf1[:, :, :], a["L0_gnn_coeff1"].rearrange("r b -> (r b)").partition_broadcast(P))
        note(cf2[:, :, :], a["L0_gnn_coeff2"].rearrange("r b -> (r b)").partition_broadcast(P))
        for t, s in ((key_in["dst"], a["dst"]), (key_in["src"], a["src"]), (typ_in, a["edge_type_8"]),
                     (weight, a["edge_weight"])):
            note(t[0:PF, :], s[0:PF * T].rearrange("(p t) -> p t", t=T))
            if PR:
                note(t[PF:PF + 1, 0:PR], s[PF * T:E].unsqueeze(0))
        note(attr[0:PF, :, :], a["edge_attr_8"][0:PF * T, :].rearrange("(p t) b -> p t b", t=T))
        if PR:
            note(attr[PF:PF + 1, 0:PR, :], a["edge_attr_8"][PF * T:E, :].unsqueeze(0))

        def chunk_rows(t, at, parts):
            if isinstance(at, int):
                return t[at * CH:at * CH + parts * K, :].rearrange("(p k) d -> p k d", k=K)
            return t[bass.ds(at * CH, CH), :].rearrange("(p k) d -> p k d", k=K)

        def batches(eng, do):
            with eng.Fori(0, LOOPS) as i:
                for pair in range(SLOTS // 2):
                    do([(i * SLOTS + 2 * pair + h, 2 * pair + h, P) for h in range(2)])
            left = [(n, n % SLOTS, P if n < FULL else TAILP) for n in range(LOOPS * SLOTS, CHUNKS)]
            while left:
                do(left[:2])
                left = left[2:]

        def use(slot, chunk):
            return (chunk - slot) // SLOTS if isinstance(chunk, int) else None

        @block.sync
        def _(sp):
            sp.wait_ge(cleared, 1)
            for dst, src in setup_loads:
                sp.dma_start(dst, src).then_inc(setup_in, 16)
            n = 0
            for j, name in enumerate(("dst", "src")):
                sp.wait_ge(rows_made, j + 1)
                for k in range(TB):
                    m = min(P, T - k * P)
                    sp.dma_start((rows_dst, rows_src)[j][k * P:k * P + m, :], rowblk[0:m, k, :]).then_inc(rows_out, 16)
                    n += 16
                sp.wait_ge(rows_out, n)
            for j, table in enumerate((rows_dst, rows_src)):
                with sp.Fori(0, Q // 2) as i:
                    for s in range(2):
                        sp.wait_ge(ranked, SEED + j * Q + i * 2 + s - 1)
                        sp.dma_start(rows[s][:, :], table[bass.ds((i * 2 + s) * G, G), :]
                                     .rearrange("t p -> (t p)").partition_broadcast(P)).then_inc(rank_rows[s], 16)
            sp.wait_ge(ranked, SEED + 2 * Q)

            for n, q in enumerate(passes):
                if q["kind"] == "node":
                    if n:
                        for s in range(2):
                            sp.wait_ge(scattered[s].sem, scattered[s].at[n])
                    last = "biased" if does_mm(q) else "normed"
                    last = "completed" if q["add"] else last

                    def load(group):
                        for ch, s, parts in group:
                            sp.wait_ge(c[last].sem, item(last, n, ch - SLOTS + 1))
                            sp.dma_start(in1[s][0:parts, :, :], chunk_rows(q["src"], ch, parts)
                                         ).then_inc(loaded[s].sem, 16)
                            if q["src2"] is not None:
                                sp.dma_start(in2[s][0:parts, :, :], chunk_rows(q["src2"], ch, parts)
                                             ).then_inc(loaded[s].sem, 16)

                    batches(sp, load)
                else:
                    table = rows_dst if q["by"] == "dst" else rows_src
                    tgt = target[q["by"]]

                    def load_group(g, s):
                        sp.wait_ge(c["x_used"].sem, item("x_used", n, g - 1))
                        sp.dma_start(gidx[s][:, :, :], ends[:, bass.ds(g, 1), :, :].rearrange("p a e t -> p (a e) t")
                                     ).then_inc(gidx_in[s].sem, 16)
                        sp.wait_ge(c["compared"].sem, item("compared", n, g - 1))
                        sp.dma_start(rows[s][:, :], table[bass.ds(g * G, G), :]
                                     .rearrange("t p -> (t p)").partition_broadcast(P)).then_inc(rows_in[s].sem, 16)

                    def load_targets(g, s, i):
                        sp.wait_ge(scattered[s].sem, scattered[s].at[n] + 16 * G * i)
                        sp.dma_start(sidx[s][:, :], tgt[:, bass.ds(g * G, G)]).then_inc(sidx_in[s].sem, 16)

                    load_group(0, 0)
                    with sp.Fori(0, Q // 2 - 1) as i:
                        load_group(i * 2 + 1, 1)
                        load_targets(i * 2, 0, i)
                        load_group(i * 2 + 2, 0)
                        load_targets(i * 2 + 1, 1, i)
                    load_group(Q - 1, 1)
                    load_targets(Q - 2, 0, Q // 2 - 1)
                    load_targets(Q - 1, 1, Q // 2 - 1)


        @block.gpsimd
        def _(pool):
            nc.gpsimd.memset(ident[:, :], 0.0).then_inc(made, 1)
            nc.gpsimd.memset(earlier[:, :, :], 1.0).then_inc(made, 1)
            nc.gpsimd.memset(epst[:, :], EPS).then_inc(made, 1)
            nc.gpsimd.memset(zero[:, :, :], 0.0).then_inc(made, 1)
            pool.wait_ge(made, 4)
            nc.gpsimd.affine_select(out=ident[:, :], in_=ident[:, :], compare_op=ALU.not_equal, fill=1.0, base=0,
                                    pattern=[[-1, P]], channel_multiplier=1).then_inc(made, 1)
            for k in range(G):
                nc.gpsimd.affine_select(out=earlier[:, k, :], in_=earlier[:, k, :], compare_op=ALU.is_gt, fill=0.0,
                                        base=k * P, pattern=[[-1, W]], channel_multiplier=1).then_inc(made, 1)
            nc.gpsimd.iota(spare[:, :, :], pattern=[[0, Q], [P, G]], base=N, channel_multiplier=1).then_inc(made, 1)
            for t, x in spare_writes:
                pool.dma_start(t[N:N + W, :].rearrange("(p k) d -> p k d", k=G), zero[:, :, :]).then_inc(x.sem, 16)

            for n, q in enumerate(passes):
                if q["kind"] == "node":
                    ready = {"o1": "normed" if not does_mm(q) else "doubled" if q["tanh"] else
                             "completed" if q["add"] else "biased",
                             "o2": "tanhed" if q["tanh"] else "normed"}
                    buf = {"o1": o1, "o2": o2}

                    def store(group):
                        for ch, s, parts in group:
                            for t, o in q["outs"]:
                                pool.wait_ge(c[ready[o]].sem, item(ready[o], n, ch + 1))
                                pool.sem_inc(pool_past, 1)
                                pool.dma_start(chunk_rows(t, ch, parts), buf[o][s][0:parts, :, :]
                                               ).then_inc(stored[s].sem, 16)

                    batches(pool, store)
                else:
                    for s in range(SLOTS):
                        pool.wait_ge(stored[s].sem, stored[s].at[n])
                    ends_of = 1 if q["kind"] == "rel" else 2

                    def gather(g, s, i):
                        pool.wait_ge(c["x_used"].sem, item("x_used", n, g - 1))
                        pool.sem_inc(pool_past, 1)
                        pool.wait_ge(gidx_in[s].sem, gidx_in[s].at[n] + 16 * (i + 1))
                        pool.sem_inc(pool_past, 1)
                        for e in range(ends_of):
                            for k in range(G):
                                pool.indirect_dma_start(
                                    out=X[s][:, k, e, :], out_offset=None, in_=q["table"][0:N, :],
                                    in_offset=bass.IndirectOffsetOnAxis(ap=gidx[s][:, e, k:k + 1], axis=0),
                                ).then_inc(gathered[s].sem, 16)

                    def scatter(g, s, i):
                        pool.wait_ge(c["sum_moved"].sem, item("sum_moved", n, g + 1))
                        pool.sem_inc(pool_past, 1)
                        pool.wait_ge(sidx_in[s].sem, sidx_in[s].at[n] + 16 * (i + 1))
                        pool.sem_inc(pool_past, 1)
                        pool.wait_ge(scattered[1 - s].sem, scattered[1 - s].at[n] + 16 * G * (i + s))
                        pool.sem_inc(pool_past, 1)
                        for k in range(G):
                            pool.indirect_dma_start(
                                out=q["to"][:, :], out_offset=bass.IndirectOffsetOnAxis(ap=sidx[s][:, k:k + 1], axis=0),
                                in_=sums[s][:, k, :], in_offset=None, compute_op=ALU.add,
                            ).then_inc(scattered[s].sem, 16)

                    gather(0, 0, 0)
                    with pool.Fori(0, Q // 2 - 1) as i:
                        gather(i * 2 + 1, 1, i)
                        scatter(i * 2, 0, i)
                        gather(i * 2 + 2, 0, i + 1)
                        scatter(i * 2 + 1, 1, i)
                    gather(Q - 1, 1, Q // 2 - 1)
                    scatter(Q - 2, 0, Q // 2 - 1)
                    scatter(Q - 1, 1, Q // 2 - 1)
            for s in range(SLOTS):
                pool.wait_ge(stored[s].sem, stored[s].total)

        by_dve = ["activated", "added", "summed", "averaged", "centered", "sq_summed", "inverted", "normed",
                  "biased", "completed", "compared", "hid_biased", "expanded", "msg_biased", "edge_term",
                  "edge_biased", "hid_summed"]
        by_act = ["squared", "rooted", "doubled", "moved", "tanhed", "pair_moved", "exp_moved", "msg_moved",
                  "sumT_moved", "sum_moved", "x_used"]
        by_pe = ["transposed", "multiplied", "pair_transposed", "hid_ready", "exp_transposed", "msg_ready",
                 "sumT_ready", "sum_ready"]

        def bc_d(t):
            return t.unsqueeze(2).to_broadcast([P, t.shape[1], D])

        def bc_k(t, k):
            return t.unsqueeze(1).to_broadcast([P, k, D])

        @block.vector
        def _(dve):
            vec = nc.vector
            for name in by_dve:
                dve.sem_inc(c[name].sem, SEED)
            dve.sem_inc(ranked, SEED)
            done = [0]

            def link(ins):
                done[0] += 1
                ins.then_inc(step, 1)
                dve.wait_ge(step, done[0])

            for t in [loop1, loop2, ppw, *wna, weight, *sums, *X, *in1, *in2]:
                link(vec.memset(t[:], 0.0))
            link(vec.memset(attr[:, :, :], 0.0))
            for t in (*key_in.values(), typ_in):
                link(vec.memset(t[:, :], PAD))
            dve.sem_inc(cleared, 1)
            dve.wait_ge(setup_in, 16 * len(setup_loads))
            dve.wait_ge(made, 10)
            for e, name in enumerate(("src", "dst")):
                link(vec.tensor_copy(key[name][:, :], key_in[name][:, :]))
                link(vec.scalar_tensor_tensor(out=ends[:, :, e, :], in0=key[name].rearrange("p (q t) -> p q t", t=G),
                                              scalar=float(N), in1=key[name].rearrange("p (q t) -> p q t", t=G),
                                              op0=ALU.is_lt, op1=ALU.mult))
            link(vec.tensor_copy(work[:, :], typ_in[:, :]))
            for r in range(R):
                link(vec.tensor_scalar(coef3[:, :, r], work[:, :], float(r), None, ALU.is_equal))
            for cf, coef in ((cf1, coef1), (cf2, coef2)):
                for b in range(NB):
                    link(vec.tensor_scalar(coef[:, :, b], coef3[:, :, 0], cf[:, 0, b:b + 1], None, ALU.mult))
                    for r in range(1, R):
                        link(vec.scalar_tensor_tensor(out=coef[:, :, b], in0=coef3[:, :, r], scalar=cf[:, r, b:b + 1],
                                                      in1=coef[:, :, b], op0=ALU.mult, op1=ALU.add))
            link(vec.tensor_tensor(coef3[:, :, :], coef3[:, :, :], weight.unsqueeze(2).to_broadcast([P, T, R]),
                                   ALU.mult))
            for b in range(R):
                link(vec.tensor_copy(piw2b[:, b, :], piw2.rearrange("f (c b) -> f c b", b=R)[:, :, b]))
            for l in range(3):
                link(vec.tensor_copy(wet_in[:, l, :], we_in[l][:, 2 * D:2 * D + 1].to_broadcast([D, P])))
            dve.sem_inc(weights_in, 1)
            dve.wait_ge(product, 1)
            for l in range(3):
                link(vec.tensor_copy(we[l][:, :], tp[0][:, l * D:(l + 1) * D]))
                link(vec.tensor_copy(wet[l][:, :], tp[0][:, (3 + l) * D:(4 + l) * D]))
            dve.wait_ge(product, 2)
            for l in range(3):
                link(vec.tensor_copy(wna[l][0:D, 0:D], tp[1][0:D, l * D:(l + 1) * D]))
                link(vec.tensor_copy(wna[l][D:P, D:P], tp[1][D:P, l * D:(l + 1) * D]))
                link(vec.tensor_copy(wnb[l][:, :], tp[1][0:D, (3 + l) * D:(4 + l) * D]))
            dve.wait_ge(product, 3)
            link(vec.tensor_copy(piw2t[:, :, :].rearrange("p b d -> p (b d)"), mm[0][0:D, 0:W]))
            dve.sem_inc(turned, 1)
            dve.wait_ge(product, 4)
            link(vec.tensor_copy(fold[:, :, :].rearrange("p k d -> p (k d)"), mm[1][:, 0:R // 2 * D]))
            for j, name in enumerate(("dst", "src")):
                dve.wait_ge(product, 5 + j)
                if j:
                    dve.wait_ge(rows_out, 16 * TB)
                for k in range(TB):
                    m = min(P, T - k * P)
                    link(vec.tensor_copy(rowblk[0:m, k, :], tp[j][0:m, k * P:(k + 1) * P]))
                dve.sem_inc(rows_made, 1)
            for j, name in enumerate(("dst", "src")):
                with dve.Fori(0, Q // 2) as i:
                    for s in range(2):
                        g = i * 2 + s
                        dve.wait_ge(rank_rows[s], 16 * (j * (Q // 2) + i + 1))
                        for k in range(G):
                            last = vec.scalar_tensor_tensor(
                                out=same[s][:, k, :], in0=rows[s][:, :], scalar=key[name][:, bass.ds(g * G + k, 1)],
                                in1=earlier[:, k, :], op0=ALU.is_equal, op1=ALU.mult, accum_out=cnt[s][:, k:k + 1])
                        last.then_inc(ranked, 1)
                        dve.wait_ge(ranked, SEED + j * Q + g + 1)
                        vec.tensor_copy(before[:, bass.ds(g * G, G)], cnt[s][:, :]).then_inc(noted, 1)
                dve.wait_ge(noted, (j + 1) * Q)
                tgt = target[name]
                link(vec.tensor_scalar(work[:, :], key[name][:, :], float(N), None, ALU.is_ge))
                link(vec.scalar_tensor_tensor(out=before[:, :], in0=before[:, :], scalar=0.5, in1=work[:, :],
                                              op0=ALU.is_gt, op1=ALU.max))
                link(vec.tensor_tensor(work[:, :], spare.rearrange("p q t -> p (q t)"), key[name][:, :], ALU.subtract))
                link(vec.tensor_tensor(work[:, :], work[:, :], before[:, :], ALU.mult))
                link(vec.tensor_tensor(tgt[:, :], work[:, :], key[name][:, :], ALU.add))
            dve.sem_inc(setup_done, 1)

            for n, q in enumerate(passes):
                def after(name, cnt_, n=n):
                    dve.wait_ge(c[name].sem, item(name, n, cnt_))

                def sig(ins, name):
                    ins.then_inc(c[name].sem, 1)

                if q["kind"] == "node":
                    if n:
                        for s in range(2):
                            dve.wait_ge(scattered[s].sem, scattered[s].at[n])
                    prep = q["prep"]
                    n_in = 1 + (q["src2"] is not None)

                    def chunks(group, q=q, n=n, prep=prep, n_in=n_in):
                        def arrived(ch, s):
                            dve.wait_ge(loaded[s].sem, loaded[s].at[n] + 16 * n_in * ((ch - s) // SLOTS + 1))

                        def free(s, ch):
                            dve.wait_ge(stored[s].sem, stored[s].at[n] + 16 * len(q["outs"]) * ((ch - s) // SLOTS))

                        if prep in ("leaky", "leaky add norm"):
                            for ch, s, _ in group:
                                arrived(ch, s)
                                if does_mm(q):
                                    after("transposed", ch - 1)
                                sig(vec.scalar_tensor_tensor(out=v[s % 2][:, :, :], in0=in1[s][:, :, :], scalar=SLOPE,
                                                             in1=in1[s][:, :, :], op0=ALU.mult, op1=ALU.max),
                                    "activated")
                        if prep == "leaky add norm":
                            for ch, s, _ in group:
                                after("activated", ch + 1)
                                sig(vec.tensor_tensor(in1[s][:, :, :], v[s % 2][:, :, :], in2[s][:, :, :], ALU.add),
                                    "added")
                        if "norm" in prep:
                            for ch, s, _ in group:
                                if prep == "norm":
                                    arrived(ch, s)
                                else:
                                    after("added", ch + 1)
                                sig(vec.tensor_reduce(stat[s][:, 0, :], in1[s][:, :, :], AX.X, ALU.add), "summed")
                            for ch, s, _ in group:
                                after("summed", ch + 1)
                                sig(vec.tensor_scalar(stat[s][:, 1, :], stat[s][:, 0, :], -1.0 / D, None, ALU.mult),
                                    "averaged")
                            for ch, s, _ in group:
                                after("averaged", ch + 1)
                                sig(vec.tensor_tensor(in1[s][:, :, :], in1[s][:, :, :], bc_d(stat[s][:, 1, :]),
                                                      ALU.add), "centered")
                            for ch, s, _ in group:
                                after("squared", ch + 1)
                                sig(vec.tensor_reduce(stat[s][:, 2, :],
                                                      sq[s % 2].rearrange("p (k d) -> p k d", d=D), AX.X, ALU.add),
                                    "sq_summed")
                            for ch, s, _ in group:
                                after("rooted", ch + 1)
                                sig(vec.reciprocal(stat[s][:, 4, :], stat[s][:, 3, :]), "inverted")
                            for ch, s, _ in group:
                                after("inverted", ch + 1)
                                if q["tanh"]:
                                    to = v[s % 2]
                                    after("transposed", ch - 1)
                                    after("doubled", ch - 1)
                                else:
                                    to = o2[s] if does_mm(q) else o1[s]
                                    free(s, ch)
                                sig(vec.tensor_tensor(to[:, :, :], in1[s][:, :, :], bc_d(stat[s][:, 4, :]), ALU.mult),
                                    "normed")
                        if does_mm(q):
                            for ch, s, _ in group:
                                after("multiplied", ch + 1)
                                free(s, ch)
                                to = o2[s] if q["tanh"] else o1[s]
                                sig(vec.tensor_tensor(to[:, :, :],
                                                      mm[s % 2].rearrange("p (k d) -> p k d", d=D),
                                                      bc_k(bias[q["shift"]][:, :], K), ALU.add), "biased")
                        if q["add"]:
                            for ch, s, _ in group:
                                after("biased", ch + 1)
                                sig(vec.tensor_tensor(o1[s][:, :, :], o1[s][:, :, :], in2[s][:, :, :], ALU.add),
                                    "completed")

                    batches(dve, chunks)
                else:
                    for s in range(SLOTS):
                        dve.wait_ge(stored[s].sem, stored[s].at[n])
                    ends_of = 1 if q["kind"] == "rel" else 2
                    tok = key[q["by"]]
                    with dve.Fori(0, Q // 2) as i:
                        for s in range(2):
                            g = i * 2 + s
                            dve.wait_ge(rows_in[s].sem, rows_in[s].at[n] + 16 * (i + 1))
                            after("sum_ready", g - 1)
                            for k in range(G):
                                last = vec.tensor_scalar(same[s][:, k, :], rows[s][:, :],
                                                         tok[:, bass.ds(g * G + k, 1)], None, ALU.is_equal)
                            sig(last, "compared")
                            if q["kind"] == "mlp":
                                after("msg_moved", g)
                                sig(vec.tensor_tensor(hid[:, :, :], bc_k(wet[q["layer"]][:, :], G),
                                                      bc_d(weight[:, bass.ds(g * G, G)]), ALU.mult), "edge_term")
                                after("edge_term", g + 1)
                                sig(vec.tensor_tensor(hid[:, :, :], hid[:, :, :],
                                                      bc_k(bias[f"L2_gnn_be{q['layer']}"][:, :], G), ALU.add),
                                    "edge_biased")
                            dve.wait_ge(gathered[s].sem, gathered[s].at[n] + 16 * G * ends_of * (i + 1))
                            if q["act"]:
                                x = X[s][:, :, 0:ends_of, :]
                                sig(vec.scalar_tensor_tensor(out=x, in0=x, scalar=SLOPE, in1=x, op0=ALU.mult,
                                                             op1=ALU.max), "activated")
                                after("activated", g + 1)
                            if q["kind"] == "pair":
                                after("hid_ready", g + 1)
                                after("expanded", g)
                                sig(vec.tensor_tensor(hid[:, :, :], ps_hid.rearrange("p (k d) -> p k d", d=D),
                                                      bc_k(bias["L1_gnn_pi_b1"][:, :], G), ALU.add), "hid_biased")
                                after("hid_biased", g + 1)
                            if q["kind"] in ("rel", "pair"):
                                after("exp_transposed", g)
                                for k in range(G):
                                    x = hid[:, k, :] if q["kind"] == "pair" else X[s][:, k, 0, :]
                                    y = Y[:, k * q["terms"] * D:(k + 1) * q["terms"] * D].rearrange("p (r d) -> p r d", d=D)
                                    cf = q["coef"][:, bass.ds(g * G + k, 1), :].rearrange("p a r -> p (a r)")
                                    last = vec.tensor_tensor(y, bc_k(x, q["terms"]), bc_d(cf), ALU.mult)
                                sig(last, "expanded")
                            if q["kind"] == "pair":
                                after("msg_ready", g + 1)
                                sig(vec.tensor_tensor(hid[:, :, :], ps_msg.rearrange("p (k d) -> p k d", d=D),
                                                      bc_k(bias["L1_gnn_ii_b"][:, :], G), ALU.add), "msg_biased")
                                after("msg_biased", g + 1)
                            if q["kind"] == "mlp":
                                after("hid_ready", g + 1)
                                after("edge_biased", g + 1)
                                sig(vec.tensor_tensor(hid[:, :, :], hid[:, :, :],
                                                      ps_hid.rearrange("p (k d) -> p k d", d=D), ALU.add),
                                    "hid_summed")
                                after("hid_summed", g + 1)
                                after("sumT_ready", g)
                                sig(vec.scalar_tensor_tensor(out=msg[:, :, :], in0=hid[:, :, :], scalar=SLOPE,
                                                             in1=hid[:, :, :], op0=ALU.mult, op1=ALU.max),
                                    "msg_moved")


        @block.scalar
        def _(act):
            sc = nc.scalar
            for name in by_act:
                if name != "x_used":
                    act.sem_inc(c[name].sem, SEED)
            act.wait_ge(setup_done, 1)
            for n, q in enumerate(passes):
                def after(name, cnt_, n=n):
                    act.wait_ge(c[name].sem, item(name, n, cnt_))

                def sig(ins, name):
                    ins.then_inc(c[name].sem, 1)

                if q["kind"] == "node":
                    def chunks(group, q=q, n=n):
                        if "norm" in q["prep"]:
                            for ch, s, _ in group:
                                after("centered", ch + 1)
                                after("sq_summed", ch - 1)
                                sig(sc.activation(sq[s % 2].rearrange("p (k d) -> p k d", d=D), in1[s][:, :, :],
                                                  ACT.Square), "squared")
                            for ch, s, _ in group:
                                after("sq_summed", ch + 1)
                                sig(sc.activation(stat[s][:, 3, :], stat[s][:, 2, :], ACT.Sqrt, bias=epst[:, :],
                                                  scale=1.0 / D), "rooted")
                        if q["tanh"]:
                            for ch, s, _ in group:
                                after("normed", ch + 1)
                                act.wait_ge(stored[s].sem, stored[s].at[n] + 32 * ((ch - s) // SLOTS))
                                sig(sc.mul(o1[s][:, :, :], v[s % 2][:, :, :], 2.0), "doubled")
                        if does_mm(q):
                            for ch, s, _ in group:
                                after("transposed", ch + 1)
                                after("multiplied", ch - 1)
                                sig(sc.copy(vT[s % 2], tp[s % 2][:, :]), "moved")
                        if q["tanh"]:
                            for ch, s, _ in group:
                                after("biased", ch + 1)
                                sig(sc.activation(o2[s][:, :, :], o2[s][:, :, :], ACT.Tanh), "tanhed")

                    batches(act, chunks)
                else:
                    with act.Fori(0, Q // 2) as i:
                        for s in range(2):
                            g = i * 2 + s
                            if q["kind"] in ("pair", "mlp"):
                                after("pair_transposed", g + 1)
                                after("hid_ready", g)
                                sig(sc.copy(XT[:, :], tp[0][:, 0:W]), "pair_moved")
                            if q["kind"] in ("rel", "pair"):
                                after("exp_transposed", g + 1)
                                after("msg_ready", g)
                                half = G * q["terms"] // 2 * P // 2
                                if half > W:
                                    sc.copy(YT[:, 0:half], tp[0][:, 0:half])
                                    sig(sc.copy(YT[:, half:2 * half], tp[1][:, 0:half]), "exp_moved")
                                else:
                                    sig(sc.copy(YT[:, 0:2 * half], tp[0][:, 0:2 * half]), "exp_moved")
                                if q["kind"] == "rel":
                                    after("msg_ready", g + 1)
                                    after("sum_ready", g)
                                    sig(sc.copy(msg[:, :, :].rearrange("p k d -> p (k d)"), ps_msg), "msg_moved")
                                else:
                                    after("msg_biased", g + 1)
                                    after("sum_ready", g)
                                    sig(sc.activation(msg[:, :, :], hid[:, :, :], ACT.Tanh), "msg_moved")
                            if q["kind"] == "mlp":
                                after("sumT_ready", g + 1)
                                after("sum_ready", g)
                                sig(sc.copy(sumT[:, :], ps_sumT), "sumT_moved")
                            after("sum_ready", g + 1)
                            act.wait_ge(scattered[s].sem, scattered[s].at[n] + 16 * G * i)
                            sig(sc.copy(sums[s][:, :, :].rearrange("p k d -> p (k d)"), ps_sum), "sum_moved")

        @block.tensor
        def _(pe):
            te = nc.tensor
            for name in by_pe:
                pe.sem_inc(c[name].sem, SEED)
            pe.sem_inc(c["x_used"].sem, SEED)
            pe.wait_ge(weights_in, 1)
            for l in range(3):
                te.transpose(tp[0][:, l * D:(l + 1) * D], we_in[l][:, 0:2 * D], ident[0:D, 0:D])
            for l in range(3):
                last = te.matmul(tp[0][:, (3 + l) * D:(4 + l) * D], wet_in[:, l, :], ident[0:D, 0:D],
                                 start=True, stop=True)
            last.then_inc(product, 1)
            for l in range(3):
                te.transpose(tp[1][:, l * D:(l + 1) * D], wna_in[l][:, :, :].rearrange("p h d -> p (h d)"),
                             ident[0:D, 0:D])
            for l in range(3):
                last = te.transpose(tp[1][:, (3 + l) * D:(4 + l) * D],
                                    wnb_in[l][:, :, :].rearrange("p h d -> p (h d)"), ident[0:D, 0:D])
            last.then_inc(product, 1)
            for b in range(R):
                last = te.transpose(mm[0][0:D, b * D:(b + 1) * D], piw2b[:, b, :], ident[0:D, 0:D])
            last.then_inc(product, 1)
            pe.wait_ge(turned, 1)
            for k in range(R // 2):
                last = te.matmul(mm[1][:, k * D:(k + 1) * D],
                                 piw2t[:, 2 * k:2 * k + 2, :].rearrange("p b d -> p (b d)"), iiw[:, :],
                                 start=True, stop=True)
            last.then_inc(product, 1)
            for j, name in enumerate(("dst", "src")):
                for k in range(TB):
                    m = min(P, T - k * P)
                    last = te.transpose(tp[j][0:m, k * P:(k + 1) * P], key[name][:, k * P:k * P + m], ident[:, :])
                last.then_inc(product, 1)
            pe.wait_ge(setup_done, 1)

            for n, q in enumerate(passes):
                def after(name, cnt_, n=n):
                    pe.wait_ge(c[name].sem, item(name, n, cnt_))

                def sig(ins, name):
                    ins.then_inc(c[name].sem, 1)

                if q["kind"] == "node":
                    if not does_mm(q):
                        continue
                    n_in = 1 + (q["src2"] is not None)

                    def chunks(group, q=q, n=n, n_in=n_in):
                        for ch, s, _ in group:
                            if q["prep"] == "none":
                                pe.wait_ge(loaded[s].sem, loaded[s].at[n] + 16 * n_in * ((ch - s) // SLOTS + 1))
                                x = in1[s]
                            elif q["prep"] == "leaky":
                                after("activated", ch + 1)
                                x = v[s % 2]
                            else:
                                after("normed", ch + 1)
                                x = v[s % 2] if q["tanh"] else o2[s]
                            after("moved", ch - 1)
                            for k in range(K // 2):
                                last = te.transpose(tp[s % 2][:, k * P:(k + 1) * P],
                                                    x[:, 2 * k:2 * k + 2, :].rearrange("p k d -> p (k d)"), ident[:, :])
                            sig(last, "transposed")
                        for ch, s, _ in group:
                            after("moved", ch + 1)
                            after("biased", ch - 1)
                            for k in range(K // 2):
                                last = te.matmul(mm[s % 2][:, k * P:(k + 1) * P], vT[s % 2][:, k * P:(k + 1) * P],
                                                 q["mat"][:, :], start=True, stop=True)
                            sig(last, "multiplied")

                    batches(pe, chunks)
                else:
                    ends_of = 1 if q["kind"] == "rel" else 2
                    with pe.Fori(0, Q // 2) as i:
                        for s in range(2):
                            g = i * 2 + s
                            if q["kind"] in ("pair", "mlp"):
                                if q["act"]:
                                    after("activated", g + 1)
                                else:
                                    pe.wait_ge(gathered[s].sem, gathered[s].at[n] + 16 * G * ends_of * (i + 1))
                                after("pair_moved", g)
                                if q["kind"] == "pair":
                                    after("exp_moved", g)
                                for k in range(G):
                                    last = te.transpose(tp[0][:, k * P:(k + 1) * P],
                                                        X[s][:, k, :, :].rearrange("p e d -> p (e d)"), ident[:, :])
                                sig(last, "pair_transposed")
                                after("pair_transposed", g + 1)
                                pe.sem_inc(c["x_used"].sem, 1)
                                w = piw1 if q["kind"] == "pair" else we[q["layer"]]
                                after("pair_moved", g + 1)
                                after("hid_biased" if q["kind"] == "pair" else "hid_summed", g)
                                for k in range(G):
                                    last = te.matmul(ps_hid[:, k * D:(k + 1) * D], XT[:, k * P:(k + 1) * P], w[:, :],
                                                     start=True, stop=True)
                                sig(last, "hid_ready")
                            if q["kind"] in ("rel", "pair"):
                                nb = q["terms"] // 2
                                after("expanded", g + 1)
                                if q["kind"] == "rel":
                                    pe.sem_inc(c["x_used"].sem, 1)
                                after("exp_moved", g)
                                for k in range(G * nb):
                                    per = 8
                                    last = te.transpose(tp[k // per][:, k % per * P:(k % per + 1) * P],
                                                        Y[:, k * P:(k + 1) * P], ident[:, :])
                                sig(last, "exp_transposed")
                                after("exp_moved", g + 1)
                                if q["kind"] == "rel":
                                    after("msg_moved", g)
                                else:
                                    after("msg_biased", g)
                                for k in range(G):
                                    for b in range(nb):
                                        last = te.matmul(ps_msg[:, k * D:(k + 1) * D],
                                                         YT[:, (k * nb + b) * P:(k * nb + b + 1) * P],
                                                         q["mat"][:, b, :], start=(b == 0), stop=(b == nb - 1))
                                sig(last, "msg_ready")
                            after("msg_moved", g + 1)
                            after("compared", g + 1)
                            if q["kind"] != "mlp":
                                after("sum_moved", g)
                                for t in range(G):
                                    for k in range(G):
                                        last = te.matmul(ps_sum[:, t * D:(t + 1) * D],
                                                         same[s][:, k, t * P:(t + 1) * P], msg[:, k, :],
                                                         start=(k == 0), stop=(k == G - 1))
                            else:
                                after("sumT_moved", g)
                                for k in range(G):
                                    last = te.matmul(ps_sumT, msg[:, k, :], same[s][:, k, :],
                                                     start=(k == 0), stop=(k == G - 1))
                                sig(last, "sumT_ready")
                                after("sumT_moved", g + 1)
                                after("sum_moved", g)
                                for k in range(G):
                                    last = te.matmul(ps_sum[:, k * D:(k + 1) * D], sumT[:, k * P:(k + 1) * P],
                                                     wnb[q["layer"]][:, :], start=True, stop=True)
                            sig(last, "sum_ready")


_INS = ["x", "src", "dst", "edge_attr_8", "edge_type_8", "edge_weight",
        "L0_gnn_basis1", "L0_gnn_coeff1", "L0_gnn_loop_w1", "L0_gnn_bias1",
        "L0_gnn_basis2", "L0_gnn_coeff2", "L0_gnn_loop_w2", "L0_gnn_bias2",
        "L1_gnn_pp_W", "L1_gnn_pp_b", "L1_gnn_pi_W1", "L1_gnn_pi_b1", "L1_gnn_pi_W2", "L1_gnn_ii_W", "L1_gnn_ii_b",
        "L2_gnn_We0", "L2_gnn_be0", "L2_gnn_Wn0", "L2_gnn_bn0", "L2_gnn_We1", "L2_gnn_be1", "L2_gnn_Wn1",
        "L2_gnn_bn1", "L2_gnn_We2", "L2_gnn_be2", "L2_gnn_Wn2", "L2_gnn_bn2", "L3_gnn_W"]


def kernel(**inputs):
    import numpy as np
    import concourse.bacc as bacc
    from concourse.bass_utils import run_bass_kernel_spmd as run

    nc = bacc.Bacc("TRN2", target_bir_lowering=False, num_devices=1)
    arrays, aps = {}, {}
    for name in _INS:
        v = np.ascontiguousarray(inputs[name])
        arrays["in_" + name] = v
        aps[name] = nc.dram_tensor("in_" + name, v.shape, mybir.dt.from_np(v.dtype), kind="ExternalInput").ap()
    shape = inputs["x"].shape
    out = nc.dram_tensor("out_x", shape, mybir.dt.float32, kind="ExternalOutput").ap()
    build(nc, aps, out)
    return run(nc, [arrays], core_ids=[0]).results[0]["out_x"]
```

```python
from collections import namedtuple
from contextlib import ExitStack

import concourse.bass as bass
from concourse import mybir

F32 = mybir.dt.float32
BF16 = mybir.dt.bfloat16
I32 = mybir.dt.int32
ALU = mybir.AluOpType
ACT = mybir.ActivationFunctionType
AX = mybir.AxisListType

P = 128
D = 64
G = 4
W = G * P
K = 16
R = 8
NB = 4
SLOTS = 4
EPS = 1e-5
SLOPE = 0.01
SEED = 6


Group = namedtuple("Group", "n s i")


def build(nc, a, out):
    N = a["x"].shape[0]
    E = a["src"].shape[0]
    Q = -(-E // (2 * W)) * 2
    T = Q * G
    PF, PR = E // T, E % T
    PAD = 1 << 20
    assert N < PAD and W >= P
    CH = P * K
    FULL = N // CH
    TAILP = (N - FULL * CH) // K
    assert FULL * CH + TAILP * K == N
    LOOPS = FULL // SLOTS
    CHUNKS = FULL + (TAILP > 0)
    TB = -(-T // P)

    ctx = ExitStack()
    with ctx:
        def sb(name, shape, dt=F32):
            return ctx.enter_context(nc.sbuf_tensor(name, shape, dt))[tuple(slice(None) for _ in shape)]

        def ps(name, shape):
            return ctx.enter_context(nc.psum_tensor(name, shape, F32))[:, :]

        def dram(name, rows, cols=D):
            return nc.dram_tensor(name, [rows, cols], F32, kind="Internal").ap()

        base1 = dram("base1", N + W)
        base2 = dram("base2", N + W)
        base3 = dram("base3", N + W)
        mlp1 = dram("mlp1", N + W)
        mlp2 = dram("mlp2", N + W)
        mlp3 = dram("mlp3", N + W)
        base4 = dram("base4", N + W)
        p1 = dram("p1", N)
        x2 = dram("x2", N)
        x3 = dram("x3", N)
        rows_dst = dram("rows_dst", T, P)
        rows_src = dram("rows_src", T, P)

        ident = sb("ident", [P, P])
        spare = sb("spare", [P, Q, G], I32)
        epst = sb("epst", [P, 1])
        zero = sb("zero", [P, G, D])
        loop1 = sb("loop1", [P, P])
        loop2 = sb("loop2", [P, P])
        ppw = sb("ppw", [P, P])
        wna = [sb(f"wna{l}", [P, P]) for l in range(3)]
        wnb = [sb(f"wnb{l}", [D, D]) for l in range(3)]
        we = [sb(f"we{l}", [P, D]) for l in range(3)]
        wet = [sb(f"wet{l}", [P, D]) for l in range(3)]
        bas1 = sb("bas1", [P, NB, D])
        bas2 = sb("bas2", [P, NB, D])
        w3 = sb("w3", [P, R, D])
        piw1 = sb("piw1", [P, D])
        fold = sb("fold", [D, R, D])
        pib1 = sb("pib1", [D, 1])
        names = ["L0_gnn_bias1", "L0_gnn_bias2", "L1_gnn_pp_b", "L1_gnn_ii_b",
                 "L2_gnn_be0", "L2_gnn_be1", "L2_gnn_be2", "L2_gnn_bn0", "L2_gnn_bn1", "L2_gnn_bn2"]
        bias = {n: sb("b_" + n, [P, D]) for n in names}
        iiw = sb("iiw", [D, D])
        piw2 = sb("piw2", [D, D * R])
        piw2b = sb("piw2b", [D, R, D])
        piw2t = sb("piw2t", [D, R, D])
        we_in = [sb(f"we_in{l}", [D, 2 * D + 1]) for l in range(3)]
        wet_in = sb("wet_in", [D, 3, P])
        wna_in = [sb(f"wna_in{l}", [D, 2, D]) for l in range(3)]
        wnb_in = [sb(f"wnb_in{l}", [D, 2, D]) for l in range(3)]
        cf1 = sb("cf1", [P, R, NB])
        cf2 = sb("cf2", [P, R, NB])

        key_in = {"dst": sb("dst_in", [P, T], I32), "src": sb("src_in", [P, T], I32)}
        typ_in = sb("typ_in", [P, T], I32)
        key = {"dst": sb("key_dst", [P, T]), "src": sb("key_src", [P, T])}
        ends = sb("ends", [P, Q, 2, G], I32)
        target = {"dst": sb("target_dst", [P, T], I32), "src": sb("target_src", [P, T], I32)}
        before = sb("before", [P, T])
        work = sb("work", [P, T])
        weight = sb("weight", [P, T])
        attr = sb("attr", [P, T, R])
        coef1 = sb("coef1", [P, T, NB])
        coef2 = sb("coef2", [P, T, NB])
        coef3 = sb("coef3", [P, T, R])
        rowblk = sb("rowblk", [P, TB, P])

        rows = [sb(f"rows{s}", [P, W]) for s in range(2)]
        gidx = [sb(f"gidx{s}", [P, 2, G], I32) for s in range(2)]
        sidx = [sb(f"sidx{s}", [P, G], I32) for s in range(2)]
        X = [sb(f"X{s}", [P, G, 2, D]) for s in range(2)]
        X1 = [x.rearrange("p k e d -> p (k e) d")[:, 0:G, :] for x in X]
        same = [sb(f"same{s}", [P, G, W]) for s in range(2)]
        cnt = [sb(f"cnt{s}", [P, G]) for s in range(2)]
        same_b = [sb(f"same_b{s}", [P, G, W], BF16) for s in range(2)]
        XT = sb("XT", [P, W])
        hidT = sb("hidT", [D, W])
        hid = sb("hid", [P, G, D])
        raw = sb("raw", [P, G, D])
        rest = sb("rest", [P, G, D])
        parts = [sb(f"parts{s}", [P, G, 3, D], BF16) for s in range(2)]
        msg = sb("msg", [P, G, D])
        sumT = sb("sumT", [D, W])
        sums = [sb(f"sums{s}", [P, G, D]) for s in range(2)]
        big = [sb(f"big{s}", [P, 2 * K * D]) for s in range(2)]
        earlier = big[0].rearrange("p (k w) -> p k w", k=G)
        terms = big[0].rearrange("p (k c) -> p k c", k=G)

        in1 = [sb(f"in1_{s}", [P, K, D]) for s in range(SLOTS)]
        in2 = [sb(f"in2_{s}", [P, K, D]) for s in range(SLOTS)]
        v = [sb(f"v{s}", [P, K, D]) for s in range(2)]
        vT = [big[s][:, 0:K * D] for s in range(2)]
        sq = [big[s][:, K * D:2 * K * D] for s in range(2)]
        o1 = [sb(f"o1_{s}", [P, K, D]) for s in range(2)] + [
            x.rearrange("p k w -> p (k w)").bitcast(F32).rearrange("p (k d) -> p k d", d=D) for x in same_b]
        o2 = [same[s // 2][:, 2 * (s % 2):2 * (s % 2) + 2, :].rearrange("p a (b d) -> p (a b) d", d=D)
              for s in range(SLOTS)]
        stat = [sb(f"stat{s}", [P, 5, K]) for s in range(SLOTS)]

        spread = ps("spread", [P, 4 * W])
        tp = [spread[:, 2 * W * s:2 * W * (s + 1)] for s in range(2)]
        mm = [ps(f"mm{s}", [P, 2 * W]) for s in range(2)]
        ps_hid = mm[0][:, 0:G * D]
        ps_hidT = mm[0][0:D, 0:W]
        ps_pair = mm[0][:, W:2 * W]
        ps_terms = spread.rearrange("p (k c) -> p k c", k=G)
        ps_parts = mm[1].rearrange("p (k c) -> p k c", k=G)[:, :, 0:3 * D]
        ps_sumT = tp[1][0:D, 0:W]
        ps_sum = mm[1][:, W:W + G * D]

        def node(src, prep, outs, mat=None, shift=None, src2=None, add=False, tanh=False):
            return dict(kind="node", src=src, src2=src2, prep=prep, mat=mat, shift=shift, add=add, tanh=tanh, outs=outs)

        def edge(kind, table, to, by="dst", **more):
            return dict(kind=kind, table=table, to=to, by=by, behind={"mlp": 2, "rel": 3, "pair": 4}[kind], **more)

        passes = [
            node(a["x"], "none", [(base1, "o1")], loop1, "L0_gnn_bias1"),
            edge("rel", a["x"], base1, coef=coef1, mat=bas1, terms=NB, act=False),
            node(base1, "leaky", [(base2, "o1")], loop2, "L0_gnn_bias2", src2=a["x"], add=True),
            edge("rel", base1, base2, coef=coef2, mat=bas2, terms=NB, act=True),
            node(base2, "norm", [(base3, "o1"), (p1, "o2")], ppw, "L1_gnn_pp_b", tanh=True),
            edge("pair", p1, base3, by="src", coef=attr, mat=fold, terms=R, act=False),
            node(base3, "norm", [(mlp1, "o1"), (x2, "o2")], wna[0], "L2_gnn_bn0"),
            edge("mlp", x2, mlp1, layer=0, act=False),
            node(mlp1, "leaky", [(mlp2, "o1")], wna[1], "L2_gnn_bn1"),
            edge("mlp", mlp1, mlp2, layer=1, act=True),
            node(mlp2, "leaky", [(mlp3, "o1")], wna[2], "L2_gnn_bn2"),
            edge("mlp", mlp2, mlp3, layer=2, act=True),
            node(mlp3, "leaky add norm", [(x3, "o1"), (base4, "o1")], src2=x2),
            edge("rel", x3, base4, coef=coef3, mat=w3, terms=R, act=False),
            node(base4, "norm", [(out, "o1")]),
        ]

        def sem(name):
            return ctx.enter_context(nc.semaphore(name))

        class Count:

            def __init__(self, name, start):
                self.sem, self.at, self.total = sem(name), [], start

        counts = {}

        def counted(name, start=SEED):
            counts[name] = Count(name, start)
            return counts[name]

        loaded = [counted(f"loaded{s}", 0) for s in range(SLOTS)]
        stored = [counted(f"stored{s}", 0) for s in range(SLOTS)]
        rows_in = [counted(f"rows_in{s}", 0) for s in range(2)]
        gidx_in = [counted(f"gidx_in{s}", 0) for s in range(2)]
        sidx_in = [counted(f"sidx_in{s}", 0) for s in range(2)]
        gathered = [counted(f"gathered{s}", 0) for s in range(2)]
        scattered = [counted(f"scattered{s}", 0) for s in range(2)]
        per_item = ["activated", "added", "summed", "averaged", "centered", "squared", "sq_summed",
                    "rooted", "inverted", "normed", "doubled", "transposed", "moved", "multiplied", "biased",
                    "completed", "tanhed",
                    "compared", "x_used", "pair_transposed", "pair_moved", "hid_ready", "hid_moved", "terms_ready",
                    "weighted", "reduced", "msg_biased", "msg_made", "high_made", "rest_made", "mid_made",
                    "parts_made", "msg_moved", "edge_term", "edge_biased", "hid_summed", "sumT_ready", "sumT_moved", "sum_ready", "sum_moved"]
        c = {n: counted(n) for n in per_item}
        pool_past = sem("pool_past")
        seeded = sem("seeded")

        def does_mm(q):
            return q["mat"] is not None

        for q in passes:
            for x in counts.values():
                x.at.append(x.total)
            if q["kind"] == "node":
                for s in range(SLOTS):
                    n = len([i for i in range(CHUNKS) if i % SLOTS == s])
                    loaded[s].total += 16 * n * (1 + (q["src2"] is not None))
                    stored[s].total += 16 * n * len(q["outs"])
                used = {"none": [], "leaky": ["activated"],
                        "norm": ["summed", "averaged", "centered", "squared", "sq_summed", "rooted", "inverted",
                                 "normed"],
                        "leaky add norm": ["activated", "added", "summed", "averaged", "centered", "squared",
                                           "sq_summed", "rooted", "inverted", "normed"]}[q["prep"]]
                used = used + (["transposed", "moved", "multiplied", "biased"] if does_mm(q) else [])
                used = used + (["completed"] if q["add"] else []) + (["doubled", "tanhed"] if q["tanh"] else [])
                for n in used:
                    c[n].total += CHUNKS
            else:
                ends_of = 1 if q["kind"] == "rel" else 2
                for s in range(2):
                    rows_in[s].total += 16 * (Q // 2)
                    gidx_in[s].total += 16 * (Q // 2)
                    sidx_in[s].total += 16 * (Q // 2)
                    gathered[s].total += 16 * G * ends_of * (Q // 2)
                    scattered[s].total += 16 * G * (Q // 2)
                used = ["compared", "x_used", "sum_ready", "sum_moved"] + (["activated"] if q["act"] else [])
                used += ["pair_transposed", "pair_moved"]
                if q["kind"] in ("rel", "pair"):
                    used += ["terms_ready", "weighted", "reduced", "high_made", "rest_made", "mid_made", "parts_made"]
                if q["kind"] in ("pair", "mlp"):
                    used += ["hid_ready"]
                if q["kind"] == "pair":
                    used += ["hid_moved", "msg_biased", "msg_made"]
                if q["kind"] == "mlp":
                    used += ["edge_term", "edge_biased", "hid_summed", "msg_moved", "sumT_ready", "sumT_moved"]
                for n in used:
                    c[n].total += Q
        spare_writes = list(zip([base1, base2, base3, mlp1, mlp2, mlp3, base4],
                                [stored[0], stored[1], stored[2], stored[3], scattered[0], scattered[1], scattered[1]]))
        for _, x in spare_writes:
            x.total += 16
            x.at = [n + 16 for n in x.at]

        def item(name, i, n):
            return c[name].at[i] + n

        def end_of_pass(counter, i):
            return counter.at[i + 1] if i + 1 < len(passes) else counter.total

        setup_in = sem("setup_in")
        cleared = sem("cleared")
        made = sem("made")
        step = sem("step")
        product = sem("product")
        rows_out = sem("rows_out")
        ranked = sem("ranked")
        rank_rows = [sem(f"rank_rows{s}") for s in range(2)]
        noted = sem("noted")

        rows_made = sem("rows_made")
        weights_in = sem("weights_in")
        turned = sem("turned")
        setup_done = sem("setup_done")
        block = ctx.enter_context(nc.Block())

        setup_loads = []

        def note(dst, src):
            setup_loads.append((dst, src))

        for t, w in ((loop1, a["L0_gnn_loop_w1"]), (loop2, a["L0_gnn_loop_w2"]), (ppw, a["L1_gnn_pp_W"])):
            note(t[0:D, 0:D], w[:, :])
            note(t[D:P, D:P], w[:, :])
        for t, w in ((bas1, a["L0_gnn_basis1"]), (bas2, a["L0_gnn_basis2"]), (w3, a["L3_gnn_W"])):
            for h in range(2):
                note(t[h * D:(h + 1) * D, :, :], w.rearrange("r i o -> i r o"))
        note(pib1, a["L1_gnn_pi_b1"].unsqueeze(1))
        note(piw1[:, :], a["L1_gnn_pi_W1"][:, :])
        note(piw2[:, :], a["L1_gnn_pi_W2"][:, :])
        note(iiw[:, :], a["L1_gnn_ii_W"][:, :])
        for l in range(3):
            note(we_in[l][:, :], a[f"L2_gnn_We{l}"][:, :])
            for h in range(2):
                note(wna_in[l][:, h, :], a[f"L2_gnn_Wn{l}"][:, 0:D])
                note(wnb_in[l][:, h, :], a[f"L2_gnn_Wn{l}"][:, D:2 * D])
        for n in names:
            note(bias[n][:, :], a[n].partition_broadcast(P))
        note(cf1[:, :, :], a["L0_gnn_coeff1"].rearrange("r b -> (r b)").partition_broadcast(P))
        note(cf2[:, :, :], a["L0_gnn_coeff2"].rearrange("r b -> (r b)").partition_broadcast(P))
        for t, s in ((key_in["dst"], a["dst"]), (key_in["src"], a["src"]), (typ_in, a["edge_type_8"]),
                     (weight, a["edge_weight"])):
            note(t[0:PF, :], s[0:PF * T].rearrange("(p t) -> p t", t=T))
            if PR:
                note(t[PF:PF + 1, 0:PR], s[PF * T:E].unsqueeze(0))
        note(attr[0:PF, :, :], a["edge_attr_8"][0:PF * T, :].rearrange("(p t) b -> p t b", t=T))
        if PR:
            note(attr[PF:PF + 1, 0:PR, :], a["edge_attr_8"][PF * T:E, :].unsqueeze(0))

        def chunk_rows(t, at, parts):
            if isinstance(at, int):
                return t[at * CH:at * CH + parts * K, :].rearrange("(p k) d -> p k d", k=K)
            return t[bass.ds(at * CH, CH), :].rearrange("(p k) d -> p k d", k=K)

        def batches(eng, do):
            with eng.Fori(0, LOOPS) as i:
                for pair in range(SLOTS // 2):
                    do([(i * SLOTS + 2 * pair + h, 2 * pair + h, P) for h in range(2)])
            left = [(n, n % SLOTS, P if n < FULL else TAILP) for n in range(LOOPS * SLOTS, CHUNKS)]
            while left:
                do(left[:2])
                left = left[2:]

        def behind(g, lag):
            s = (g.s - lag) % 2
            at = Group(g.n - lag, s, g.i + (g.s - lag - s) // 2)
            return None if isinstance(at.n, int) and not 0 <= at.n < Q else at

        def steps(eng, lag, do):
            peel = lag + lag % 2
            for n in range(peel):
                do(Group(n, n % 2, n // 2))
            with eng.Fori(0, (Q - peel) // 2) as i:
                for s in range(2):
                    do(Group(i * 2 + peel + s, s, i + peel // 2))
            for n in range(Q, Q + lag):
                do(Group(n, n % 2, n // 2))

        @block.sync
        def _(sp):
            sp.wait_ge(cleared, 1)
            for dst, src in setup_loads:
                sp.dma_start(dst, src).then_inc(setup_in, 16)
            n = 0
            for j, name in enumerate(("dst", "src")):
                sp.wait_ge(rows_made, j + 1)
                for k in range(TB):
                    m = min(P, T - k * P)
                    sp.dma_start((rows_dst, rows_src)[j][k * P:k * P + m, :], rowblk[0:m, k, :]).then_inc(rows_out, 16)
                    n += 16
                sp.wait_ge(rows_out, n)
            for j, table in enumerate((rows_dst, rows_src)):
                with sp.Fori(0, Q // 2) as i:
                    for s in range(2):
                        sp.wait_ge(ranked, SEED + j * Q + i * 2 + s - 1)
                        sp.dma_start(rows[s][:, :], table[bass.ds((i * 2 + s) * G, G), :]
                                     .rearrange("t p -> (t p)").partition_broadcast(P)).then_inc(rank_rows[s], 16)
            sp.wait_ge(ranked, SEED + 2 * Q)

            for n, q in enumerate(passes):
                if q["kind"] == "node":
                    if n:
                        for s in range(2):
                            sp.wait_ge(scattered[s].sem, scattered[s].at[n])
                    last = "biased" if does_mm(q) else "normed"
                    last = "completed" if q["add"] else last

                    def load(group):
                        for ch, s, parts in group:
                            sp.wait_ge(c[last].sem, item(last, n, ch - SLOTS + 1))
                            sp.dma_start(in1[s][0:parts, :, :], chunk_rows(q["src"], ch, parts)
                                         ).then_inc(loaded[s].sem, 16)
                            if q["src2"] is not None:
                                sp.dma_start(in2[s][0:parts, :, :], chunk_rows(q["src2"], ch, parts)
                                             ).then_inc(loaded[s].sem, 16)

                    batches(sp, load)
                else:
                    table = rows_dst if q["by"] == "dst" else rows_src
                    tgt = target[q["by"]]

                    def load(g, q=q, n=n, table=table, tgt=tgt):
                        now = behind(g, 0)
                        if now:
                            sp.wait_ge(c["x_used"].sem, item("x_used", n, now.n - 1))
                            sp.dma_start(gidx[now.s], ends[:, bass.ds(now.n, 1), :, :].rearrange("p a e t -> p (a e) t")
                                         ).then_inc(gidx_in[now.s].sem, 16)
                            sp.wait_ge(c["compared"].sem, item("compared", n, now.n - 1))
                            sp.dma_start(rows[now.s], table[bass.ds(now.n * G, G), :]
                                         .rearrange("t p -> (t p)").partition_broadcast(P)).then_inc(rows_in[now.s].sem, 16)
                        old = behind(g, q["behind"])
                        if old:
                            sp.wait_ge(scattered[old.s].sem, scattered[old.s].at[n] + 16 * G * old.i)
                            sp.dma_start(sidx[old.s], tgt[:, bass.ds(old.n * G, G)]).then_inc(sidx_in[old.s].sem, 16)

                    steps(sp, q["behind"], load)

        @block.gpsimd
        def _(pool):
            nc.gpsimd.memset(ident[:, :], 0.0).then_inc(made, 1)
            nc.gpsimd.memset(earlier[:, :, :], 1.0).then_inc(made, 1)
            nc.gpsimd.memset(epst[:, :], EPS).then_inc(made, 1)
            nc.gpsimd.memset(zero[:, :, :], 0.0).then_inc(made, 1)
            pool.wait_ge(made, 4)
            nc.gpsimd.affine_select(out=ident[:, :], in_=ident[:, :], compare_op=ALU.not_equal, fill=1.0, base=0,
                                    pattern=[[-1, P]], channel_multiplier=1).then_inc(made, 1)
            for k in range(G):
                nc.gpsimd.affine_select(out=earlier[:, k, :], in_=earlier[:, k, :], compare_op=ALU.is_gt, fill=0.0,
                                        base=k * P, pattern=[[-1, W]], channel_multiplier=1).then_inc(made, 1)
            nc.gpsimd.iota(spare[:, :, :], pattern=[[0, Q], [P, G]], base=N, channel_multiplier=1).then_inc(made, 1)
            for t, x in spare_writes:
                pool.dma_start(t[N:N + W, :].rearrange("(p k) d -> p k d", k=G), zero[:, :, :]).then_inc(x.sem, 16)

            for n, q in enumerate(passes):
                if q["kind"] == "node":
                    ready = {"o1": "normed" if not does_mm(q) else "doubled" if q["tanh"] else
                             "completed" if q["add"] else "biased",
                             "o2": "tanhed" if q["tanh"] else "normed"}
                    buf = {"o1": o1, "o2": o2}

                    def store(group):
                        for ch, s, parts in group:
                            for t, o in q["outs"]:
                                pool.wait_ge(c[ready[o]].sem, item(ready[o], n, ch + 1))
                                pool.sem_inc(pool_past, 1)
                                pool.dma_start(chunk_rows(t, ch, parts), buf[o][s][0:parts, :, :]
                                               ).then_inc(stored[s].sem, 16)

                    batches(pool, store)
                else:
                    for s in range(SLOTS):
                        pool.wait_ge(stored[s].sem, stored[s].at[n])
                    ends_of = 1 if q["kind"] == "rel" else 2

                    def gather(g, q=q, n=n, ends_of=ends_of):
                        pool.wait_ge(c["x_used"].sem, item("x_used", n, g.n - 1))
                        pool.sem_inc(pool_past, 1)
                        pool.wait_ge(gidx_in[g.s].sem, gidx_in[g.s].at[n] + 16 * (g.i + 1))
                        pool.sem_inc(pool_past, 1)
                        for e in range(ends_of):
                            for k in range(G):
                                pool.indirect_dma_start(
                                    out=X[g.s][:, k, e, :] if ends_of == 2 else X1[g.s][:, k, :], out_offset=None, in_=q["table"][0:N, :],
                                    in_offset=bass.IndirectOffsetOnAxis(ap=gidx[g.s][:, e, k:k + 1], axis=0),
                                ).then_inc(gathered[g.s].sem, 16)

                    def scatter(g, q=q, n=n):
                        pool.wait_ge(c["sum_moved"].sem, item("sum_moved", n, g.n + 1))
                        pool.sem_inc(pool_past, 1)
                        pool.wait_ge(sidx_in[g.s].sem, sidx_in[g.s].at[n] + 16 * (g.i + 1))
                        pool.sem_inc(pool_past, 1)
                        pool.wait_ge(scattered[1 - g.s].sem, scattered[1 - g.s].at[n] + 16 * G * (g.i + g.s))
                        pool.sem_inc(pool_past, 1)
                        for k in range(G):
                            pool.indirect_dma_start(
                                out=q["to"], out_offset=bass.IndirectOffsetOnAxis(ap=sidx[g.s][:, k:k + 1], axis=0),
                                in_=sums[g.s][:, k, :], in_offset=None, compute_op=ALU.add,
                            ).then_inc(scattered[g.s].sem, 16)

                    def fetch_and_add(g, q=q):
                        if behind(g, 0):
                            gather(g)
                        if behind(g, q["behind"]):
                            scatter(behind(g, q["behind"]))

                    steps(pool, q["behind"], fetch_and_add)
            for s in range(SLOTS):
                pool.wait_ge(stored[s].sem, stored[s].total)

        by_dve = ["activated", "added", "summed", "averaged", "centered", "sq_summed", "inverted", "normed",
                  "biased", "completed", "compared", "weighted", "reduced", "msg_biased", "rest_made", "parts_made",
                  "msg_moved", "edge_term", "edge_biased", "hid_summed"]
        by_act = ["squared", "rooted", "doubled", "moved", "tanhed", "pair_moved", "hid_moved", "msg_made",
                  "high_made", "mid_made", "sumT_moved", "sum_moved"]
        by_pe = ["transposed", "multiplied", "pair_transposed", "hid_ready", "terms_ready", "sumT_ready",
                 "sum_ready", "x_used"]

        def bc_d(t):
            return t.unsqueeze(2).to_broadcast([P, t.shape[1], D])

        def bc_k(t, k):
            return t.unsqueeze(1).to_broadcast([P, k, D])

        @block.vector
        def _(dve):
            vec = nc.vector
            for name in by_dve:
                dve.sem_inc(c[name].sem, SEED)
            dve.sem_inc(ranked, SEED)
            done = [0]

            def link(ins):
                done[0] += 1
                ins.then_inc(step, 1)
                dve.wait_ge(step, done[0])

            for t in [loop1, loop2, ppw, *wna, weight, *sums, *X, *in1, *in2]:
                link(vec.memset(t[:], 0.0))
            link(vec.memset(attr[:, :, :], 0.0))
            for t in (*key_in.values(), typ_in):
                link(vec.memset(t[:, :], PAD))
            dve.sem_inc(cleared, 1)
            dve.wait_ge(setup_in, 16 * len(setup_loads))
            dve.wait_ge(made, 10)
            for e, name in enumerate(("src", "dst")):
                link(vec.tensor_copy(key[name][:, :], key_in[name][:, :]))
                link(vec.scalar_tensor_tensor(out=ends[:, :, e, :], in0=key[name].rearrange("p (q t) -> p q t", t=G),
                                              scalar=float(N), in1=key[name].rearrange("p (q t) -> p q t", t=G),
                                              op0=ALU.is_lt, op1=ALU.mult))
            link(vec.tensor_copy(work[:, :], typ_in[:, :]))
            for r in range(R):
                link(vec.tensor_scalar(coef3[:, :, r], work[:, :], float(r), None, ALU.is_equal))
            for cf, coef in ((cf1, coef1), (cf2, coef2)):
                for b in range(NB):
                    link(vec.tensor_scalar(coef[:, :, b], coef3[:, :, 0], cf[:, 0, b:b + 1], None, ALU.mult))
                    for r in range(1, R):
                        link(vec.scalar_tensor_tensor(out=coef[:, :, b], in0=coef3[:, :, r], scalar=cf[:, r, b:b + 1],
                                                      in1=coef[:, :, b], op0=ALU.mult, op1=ALU.add))
            link(vec.tensor_tensor(coef3[:, :, :], coef3[:, :, :], weight.unsqueeze(2).to_broadcast([P, T, R]),
                                   ALU.mult))
            for b in range(R):
                link(vec.tensor_copy(piw2b[:, b, :], piw2.rearrange("f (c b) -> f c b", b=R)[:, :, b]))
            for l in range(3):
                link(vec.tensor_copy(wet_in[:, l, :], we_in[l][:, 2 * D:2 * D + 1].to_broadcast([D, P])))
            dve.sem_inc(weights_in, 1)
            dve.wait_ge(product, 1)
            for l in range(3):
                link(vec.tensor_copy(we[l][:, :], tp[0][:, l * D:(l + 1) * D]))
                link(vec.tensor_copy(wet[l][:, :], tp[0][:, (3 + l) * D:(4 + l) * D]))
            dve.wait_ge(product, 2)
            for l in range(3):
                link(vec.tensor_copy(wna[l][0:D, 0:D], tp[1][0:D, l * D:(l + 1) * D]))
                link(vec.tensor_copy(wna[l][D:P, D:P], tp[1][D:P, l * D:(l + 1) * D]))
                link(vec.tensor_copy(wnb[l][:, :], tp[1][0:D, (3 + l) * D:(4 + l) * D]))
            dve.wait_ge(product, 3)
            link(vec.tensor_copy(piw2t[:, :, :].rearrange("p b d -> p (b d)"), mm[0][0:D, 0:W]))
            dve.sem_inc(turned, 1)
            dve.wait_ge(product, 4)
            link(vec.tensor_copy(fold.rearrange("p b d -> p (b d)"), mm[1][0:D, 0:R * D]))
            for j, name in enumerate(("dst", "src")):
                dve.wait_ge(product, 5 + j)
                if j:
                    dve.wait_ge(rows_out, 16 * TB)
                for k in range(TB):
                    m = min(P, T - k * P)
                    link(vec.tensor_copy(rowblk[0:m, k, :], tp[j][0:m, k * P:(k + 1) * P]))
                dve.sem_inc(rows_made, 1)
            for j, name in enumerate(("dst", "src")):
                with dve.Fori(0, Q // 2) as i:
                    for s in range(2):
                        g = i * 2 + s
                        dve.wait_ge(rank_rows[s], 16 * (j * (Q // 2) + i + 1))
                        for k in range(G):
                            last = vec.scalar_tensor_tensor(
                                out=same[s][:, k, :], in0=rows[s][:, :], scalar=key[name][:, bass.ds(g * G + k, 1)],
                                in1=earlier[:, k, :], op0=ALU.is_equal, op1=ALU.mult, accum_out=cnt[s][:, k:k + 1])
                        last.then_inc(ranked, 1)
                        dve.wait_ge(ranked, SEED + j * Q + g + 1)
                        vec.tensor_copy(before[:, bass.ds(g * G, G)], cnt[s][:, :]).then_inc(noted, 1)
                dve.wait_ge(noted, (j + 1) * Q)
                tgt = target[name]
                link(vec.tensor_scalar(work[:, :], key[name][:, :], float(N), None, ALU.is_ge))
                link(vec.scalar_tensor_tensor(out=before[:, :], in0=before[:, :], scalar=0.5, in1=work[:, :],
                                              op0=ALU.is_gt, op1=ALU.max))
                link(vec.tensor_tensor(work[:, :], spare.rearrange("p q t -> p (q t)"), key[name][:, :], ALU.subtract))
                link(vec.tensor_tensor(work[:, :], work[:, :], before[:, :], ALU.mult))
                link(vec.tensor_tensor(tgt[:, :], work[:, :], key[name][:, :], ALU.add))
            dve.sem_inc(setup_done, 1)

            for n, q in enumerate(passes):
                def after(name, cnt_, n=n):
                    dve.wait_ge(c[name].sem, item(name, n, cnt_))

                def sig(ins, name):
                    ins.then_inc(c[name].sem, 1)

                if q["kind"] == "node":
                    if n:
                        for s in range(2):
                            dve.wait_ge(scattered[s].sem, scattered[s].at[n])
                    prep = q["prep"]
                    n_in = 1 + (q["src2"] is not None)

                    def chunks(group, q=q, n=n, prep=prep, n_in=n_in):
                        def arrived(ch, s):
                            dve.wait_ge(loaded[s].sem, loaded[s].at[n] + 16 * n_in * ((ch - s) // SLOTS + 1))

                        def free(s, ch):
                            dve.wait_ge(stored[s].sem, stored[s].at[n] + 16 * len(q["outs"]) * ((ch - s) // SLOTS))

                        if prep in ("leaky", "leaky add norm"):
                            for ch, s, _ in group:
                                arrived(ch, s)
                                if does_mm(q):
                                    after("transposed", ch - 1)
                                sig(vec.scalar_tensor_tensor(out=v[s % 2][:, :, :], in0=in1[s][:, :, :], scalar=SLOPE,
                                                             in1=in1[s][:, :, :], op0=ALU.mult, op1=ALU.max),
                                    "activated")
                        if prep == "leaky add norm":
                            for ch, s, _ in group:
                                after("activated", ch + 1)
                                sig(vec.tensor_tensor(in1[s][:, :, :], v[s % 2][:, :, :], in2[s][:, :, :], ALU.add),
                                    "added")
                        if "norm" in prep:
                            for ch, s, _ in group:
                                if prep == "norm":
                                    arrived(ch, s)
                                else:
                                    after("added", ch + 1)
                                sig(vec.tensor_reduce(stat[s][:, 0, :], in1[s][:, :, :], AX.X, ALU.add), "summed")
                            for ch, s, _ in group:
                                after("summed", ch + 1)
                                sig(vec.tensor_scalar(stat[s][:, 1, :], stat[s][:, 0, :], -1.0 / D, None, ALU.mult),
                                    "averaged")
                            for ch, s, _ in group:
                                after("averaged", ch + 1)
                                sig(vec.tensor_tensor(in1[s][:, :, :], in1[s][:, :, :], bc_d(stat[s][:, 1, :]),
                                                      ALU.add), "centered")
                            for ch, s, _ in group:
                                after("squared", ch + 1)
                                sig(vec.tensor_reduce(stat[s][:, 2, :],
                                                      sq[s % 2].rearrange("p (k d) -> p k d", d=D), AX.X, ALU.add),
                                    "sq_summed")
                            for ch, s, _ in group:
                                after("rooted", ch + 1)
                                sig(vec.reciprocal(stat[s][:, 4, :], stat[s][:, 3, :]), "inverted")
                            for ch, s, _ in group:
                                after("inverted", ch + 1)
                                if q["tanh"]:
                                    to = v[s % 2]
                                    after("transposed", ch - 1)
                                    after("doubled", ch - 1)
                                else:
                                    to = o2[s] if does_mm(q) else o1[s]
                                    free(s, ch)
                                sig(vec.tensor_tensor(to[:, :, :], in1[s][:, :, :], bc_d(stat[s][:, 4, :]), ALU.mult),
                                    "normed")
                        if does_mm(q):
                            for ch, s, _ in group:
                                after("multiplied", ch + 1)
                                free(s, ch)
                                to = o2[s] if q["tanh"] else o1[s]
                                sig(vec.tensor_tensor(to[:, :, :],
                                                      mm[s % 2].rearrange("p (k d) -> p k d", d=D),
                                                      bc_k(bias[q["shift"]][:, :], K), ALU.add), "biased")
                        if q["add"]:
                            for ch, s, _ in group:
                                after("biased", ch + 1)
                                sig(vec.tensor_tensor(o1[s][:, :, :], o1[s][:, :, :], in2[s][:, :, :], ALU.add),
                                    "completed")

                    batches(dve, chunks)
                else:
                    for s in range(SLOTS):
                        dve.wait_ge(stored[s].sem, stored[s].at[n])
                    ends_of = 1 if q["kind"] == "rel" else 2
                    tok = key[q["by"]]
                    matrix = same if q["kind"] == "mlp" else same_b

                    def compare(g, tok=tok, q=q, matrix=matrix):
                        dve.wait_ge(rows_in[g.s].sem, rows_in[g.s].at[n] + 16 * (g.i + 1))
                        after("sumT_ready" if q["kind"] == "mlp" else "sum_ready", g.n - 1)
                        for k in range(G):
                            last = vec.tensor_scalar(matrix[g.s][:, k, :], rows[g.s],
                                                     tok[:, bass.ds(g.n * G + k, 1)], None, ALU.is_equal)
                        sig(last, "compared")

                    def activate(g, q=q, ends_of=ends_of):
                        if q["act"]:
                            dve.wait_ge(gathered[g.s].sem, gathered[g.s].at[n] + 16 * G * ends_of * (g.i + 1))
                            x = X[g.s] if ends_of == 2 else X1[g.s]
                            sig(vec.scalar_tensor_tensor(out=x, in0=x, scalar=SLOPE, in1=x, op0=ALU.mult, op1=ALU.max),
                                "activated")

                    def weigh(g, q=q):
                        m = q["terms"]
                        after("terms_ready", g.n + 1)
                        after("reduced", g.n)
                        for k in (0, 2):
                            cf = q["coef"][:, bass.ds(g.n * G + k, 2), :].unsqueeze(3).to_broadcast([P, 2, m, D])
                            last = vec.tensor_tensor(
                                terms[:, k:k + 2, 0:m * D].rearrange("p k (r d) -> p k r d", d=D),
                                ps_terms[:, k:k + 2, 0:m * D].rearrange("p k (r d) -> p k r d", d=D), cf, ALU.mult)
                        sig(last, "weighted")
                        after("weighted", g.n + 1)
                        after("rest_made", g.n)
                        if q["kind"] == "pair":
                            after("msg_biased", g.n)
                        sig(vec.tensor_reduce(raw, terms[:, :, 0:m * D].rearrange("p k (r d) -> p k d r", d=D),
                                              AX.X, ALU.add), "reduced")
                        if q["kind"] == "pair":
                            after("reduced", g.n + 1)
                            after("msg_made", g.n)
                            sig(vec.tensor_tensor(hid, raw, bc_k(bias["L1_gnn_ii_b"], G), ALU.add), "msg_biased")

                    def part_rest(g, q=q):
                        m = msg if q["kind"] == "pair" else raw
                        after("high_made", g.n + 1)
                        after("parts_made", g.n)
                        sig(vec.tensor_tensor(rest, m, parts[g.s][:, :, 0, :], ALU.subtract), "rest_made")

                    def part_low(g):
                        after("mid_made", g.n + 1)
                        sig(vec.tensor_tensor(parts[g.s][:, :, 2, :], rest, parts[g.s][:, :, 1, :], ALU.subtract),
                            "parts_made")

                    def join_sums(g):
                        after("sum_ready", g.n + 1)
                        dve.wait_ge(scattered[g.s].sem, scattered[g.s].at[n] + 16 * G * g.i)
                        sig(vec.tensor_reduce(sums[g.s], ps_parts.rearrange("p k (c d) -> p k d c", d=D), AX.X,
                                              ALU.add), "sum_moved")

                    def rel(g):
                        if behind(g, 1):
                            part_rest(behind(g, 1))
                        if behind(g, 2):
                            join_sums(behind(g, 2))
                        if behind(g, 0):
                            activate(g)
                            compare(g)
                        if behind(g, 1):
                            part_low(behind(g, 1))
                        if behind(g, 0):
                            weigh(g)

                    def pair(g):
                        if behind(g, 2):
                            part_rest(behind(g, 2))
                        if behind(g, 3):
                            join_sums(behind(g, 3))
                        if behind(g, 1):
                            compare(behind(g, 1))
                        if behind(g, 2):
                            part_low(behind(g, 2))
                        if behind(g, 1):
                            weigh(behind(g, 1))

                    def mlp(g, q=q):
                        compare(g)
                        after("msg_moved", g.n)
                        sig(vec.tensor_tensor(hid, bc_k(wet[q["layer"]], G), bc_d(weight[:, bass.ds(g.n * G, G)]),
                                              ALU.mult), "edge_term")
                        after("edge_term", g.n + 1)
                        sig(vec.tensor_tensor(hid, hid, bc_k(bias[f"L2_gnn_be{q['layer']}"], G), ALU.add),
                            "edge_biased")
                        activate(g)
                        after("hid_ready", g.n + 1)
                        after("edge_biased", g.n + 1)
                        sig(vec.tensor_tensor(hid, hid, ps_hid.rearrange("p (k d) -> p k d", d=D), ALU.add),
                            "hid_summed")
                        after("hid_summed", g.n + 1)
                        after("sumT_ready", g.n)
                        sig(vec.scalar_tensor_tensor(out=msg, in0=hid, scalar=SLOPE, in1=hid, op0=ALU.mult,
                                                     op1=ALU.max), "msg_moved")

                    kind = q["kind"]
                    steps(dve, {"rel": 2, "pair": 3, "mlp": 0}[kind], {"rel": rel, "pair": pair, "mlp": mlp}[kind])

        @block.scalar
        def _(act):
            sc = nc.scalar
            for name in by_act:
                act.sem_inc(c[name].sem, SEED)
            act.wait_ge(setup_done, 1)
            for n, q in enumerate(passes):
                def after(name, cnt_, n=n):
                    act.wait_ge(c[name].sem, item(name, n, cnt_))

                def sig(ins, name):
                    ins.then_inc(c[name].sem, 1)

                if q["kind"] == "node":
                    def chunks(group, q=q, n=n):
                        if "norm" in q["prep"]:
                            for ch, s, _ in group:
                                after("centered", ch + 1)
                                after("sq_summed", ch - 1)
                                sig(sc.activation(sq[s % 2].rearrange("p (k d) -> p k d", d=D), in1[s][:, :, :],
                                                  ACT.Square), "squared")
                            for ch, s, _ in group:
                                after("sq_summed", ch + 1)
                                sig(sc.activation(stat[s][:, 3, :], stat[s][:, 2, :], ACT.Sqrt, bias=epst[:, :],
                                                  scale=1.0 / D), "rooted")
                        if q["tanh"]:
                            for ch, s, _ in group:
                                after("normed", ch + 1)
                                act.wait_ge(stored[s].sem, stored[s].at[n] + 32 * ((ch - s) // SLOTS))
                                sig(sc.mul(o1[s][:, :, :], v[s % 2][:, :, :], 2.0), "doubled")
                        if does_mm(q):
                            for ch, s, _ in group:
                                after("transposed", ch + 1)
                                after("multiplied", ch - 1)
                                sig(sc.copy(vT[s % 2], tp[s % 2][:, :]), "moved")
                        if q["tanh"]:
                            for ch, s, _ in group:
                                after("biased", ch + 1)
                                sig(sc.activation(o2[s][:, :, :], o2[s][:, :, :], ACT.Tanh), "tanhed")

                    batches(act, chunks)
                else:
                    def move_pair(g, q=q):
                        after("pair_transposed", g.n + 1)
                        after("terms_ready" if q["kind"] == "rel" else "hid_ready", g.n)
                        cols = W // 2 if q["kind"] == "rel" else W
                        sig(sc.copy(XT[:, 0:cols], ps_pair[:, 0:cols]), "pair_moved")

                    def move_hidden(g):
                        after("hid_ready", g.n + 1)
                        after("terms_ready", g.n)
                        sig(sc.activation(hidT, ps_hidT, ACT.Identity, bias=pib1), "hid_moved")

                    def part_high(g, q=q):
                        if q["kind"] == "pair":
                            after("msg_biased", g.n + 1)
                            after("rest_made", g.n)
                            sig(sc.activation(msg, hid, ACT.Tanh), "msg_made")
                            after("msg_made", g.n + 1)
                        else:
                            after("reduced", g.n + 1)
                        after("sum_ready", g.n - 1)
                        sig(sc.copy(parts[g.s][:, :, 0, :], msg if q["kind"] == "pair" else raw), "high_made")

                    def part_mid(g):
                        after("rest_made", g.n + 1)
                        sig(sc.copy(parts[g.s][:, :, 1, :], rest), "mid_made")

                    def move_sums(g):
                        after("sum_ready", g.n + 1)
                        act.wait_ge(scattered[g.s].sem, scattered[g.s].at[n] + 16 * G * g.i)
                        sig(sc.copy(sums[g.s].rearrange("p k d -> p (k d)"), ps_sum), "sum_moved")

                    def rel(g):
                        if behind(g, 1):
                            part_high(behind(g, 1))
                        if behind(g, 0):
                            move_pair(g)
                        if behind(g, 1):
                            part_mid(behind(g, 1))

                    def pair(g):
                        if behind(g, 2):
                            part_high(behind(g, 2))
                        if behind(g, 0):
                            move_pair(g)
                        if behind(g, 2):
                            part_mid(behind(g, 2))
                        if behind(g, 0):
                            move_hidden(g)

                    def mlp(g):
                        if behind(g, 0):
                            move_pair(g)
                        old = behind(g, 1)
                        if old:
                            after("sumT_ready", old.n + 1)
                            after("sum_ready", old.n)
                            sig(sc.copy(sumT, ps_sumT), "sumT_moved")
                            move_sums(old)

                    kind = q["kind"]
                    steps(act, 2 if kind == "pair" else 1, {"rel": rel, "pair": pair, "mlp": mlp}[kind])

        @block.tensor
        def _(pe):
            te = nc.tensor
            for name in by_pe:
                pe.sem_inc(c[name].sem, SEED)
            pe.wait_ge(weights_in, 1)
            for l in range(3):
                te.transpose(tp[0][:, l * D:(l + 1) * D], we_in[l][:, 0:2 * D], ident[0:D, 0:D])
            for l in range(3):
                last = te.matmul(tp[0][:, (3 + l) * D:(4 + l) * D], wet_in[:, l, :], ident[0:D, 0:D],
                                 start=True, stop=True)
            last.then_inc(product, 1)
            for l in range(3):
                te.transpose(tp[1][:, l * D:(l + 1) * D], wna_in[l][:, :, :].rearrange("p h d -> p (h d)"),
                             ident[0:D, 0:D])
            for l in range(3):
                last = te.transpose(tp[1][:, (3 + l) * D:(4 + l) * D],
                                    wnb_in[l][:, :, :].rearrange("p h d -> p (h d)"), ident[0:D, 0:D])
            last.then_inc(product, 1)
            for b in range(R):
                last = te.transpose(mm[0][0:D, b * D:(b + 1) * D], piw2b[:, b, :], ident[0:D, 0:D])
            last.then_inc(product, 1)
            pe.wait_ge(turned, 1)
            for b in range(R):
                last = te.matmul(mm[1][0:D, b * D:(b + 1) * D], piw2t[:, b, :], iiw, start=True, stop=True)
            last.then_inc(product, 1)
            for j, name in enumerate(("dst", "src")):
                for k in range(TB):
                    m = min(P, T - k * P)
                    last = te.transpose(tp[j][0:m, k * P:(k + 1) * P], key[name][:, k * P:k * P + m], ident[:, :])
                last.then_inc(product, 1)
            pe.wait_ge(setup_done, 1)

            for n, q in enumerate(passes):
                def after(name, cnt_, n=n):
                    pe.wait_ge(c[name].sem, item(name, n, cnt_))

                def sig(ins, name):
                    ins.then_inc(c[name].sem, 1)

                if q["kind"] == "node":
                    if not does_mm(q):
                        continue
                    n_in = 1 + (q["src2"] is not None)

                    def chunks(group, q=q, n=n, n_in=n_in):
                        for ch, s, _ in group:
                            if q["prep"] == "none":
                                pe.wait_ge(loaded[s].sem, loaded[s].at[n] + 16 * n_in * ((ch - s) // SLOTS + 1))
                                x = in1[s]
                            elif q["prep"] == "leaky":
                                after("activated", ch + 1)
                                x = v[s % 2]
                            else:
                                after("normed", ch + 1)
                                x = v[s % 2] if q["tanh"] else o2[s]
                            after("moved", ch - 1)
                            for k in range(K // 2):
                                last = te.transpose(tp[s % 2][:, k * P:(k + 1) * P],
                                                    x[:, 2 * k:2 * k + 2, :].rearrange("p k d -> p (k d)"), ident[:, :])
                            sig(last, "transposed")
                        for ch, s, _ in group:
                            after("moved", ch + 1)
                            after("biased", ch - 1)
                            for k in range(K // 2):
                                last = te.matmul(mm[s % 2][:, k * P:(k + 1) * P], vT[s % 2][:, k * P:(k + 1) * P],
                                                 q["mat"][:, :], start=True, stop=True)
                            sig(last, "multiplied")

                    batches(pe, chunks)
                else:
                    ends_of = 1 if q["kind"] == "rel" else 2
                    def turn_pair(g, q=q, ends_of=ends_of):
                        if q["act"]:
                            after("activated", g.n + 1)
                        else:
                            pe.wait_ge(gathered[g.s].sem, gathered[g.s].at[n] + 16 * G * ends_of * (g.i + 1))
                        after("pair_moved", g.n)
                        x = X[g.s].rearrange("p k e d -> p (k e d)")
                        for k in range(G * ends_of // 2):
                            last = te.transpose(ps_pair[:, k * P:(k + 1) * P], x[:, k * P:(k + 1) * P], ident)
                        sig(last, "pair_transposed")
                        after("pair_transposed", g.n + 1)
                        pe.sem_inc(c["x_used"].sem, 1)

                    def hidden(g, q=q):
                        after("pair_moved", g.n + 1)
                        after("hid_summed", g.n)
                        for k in range(G):
                            last = te.matmul(ps_hid[:, k * D:(k + 1) * D], XT[:, k * P:(k + 1) * P], we[q["layer"]],
                                             start=True, stop=True)
                        sig(last, "hid_ready")

                    def hidden_turned(g):
                        after("pair_moved", g.n + 1)
                        after("hid_moved", g.n)
                        sig(te.matmul(ps_hidT, piw1, XT, start=True, stop=True), "hid_ready")

                    def make_terms(g, q=q):
                        after("pair_moved" if q["kind"] == "rel" else "hid_moved", g.n + 1)
                        after("weighted", g.n)
                        mat = q["mat"].rearrange("p r d -> p (r d)")
                        for k in range(G):
                            if q["kind"] == "rel":
                                h = k % 2 * D
                                x, w = XT[h:h + D, k // 2 * P:(k // 2 + 1) * P], mat[h:h + D, :]
                            else:
                                x, w = hidT[:, k * P:(k + 1) * P], mat
                            last = te.matmul(ps_terms[:, k, 0:q["terms"] * D], x, w, start=True, stop=True)
                        sig(last, "terms_ready")

                    def add_up(g):
                        after("parts_made", g.n + 1)
                        after("compared", g.n + 1)
                        after("sum_moved", g.n)
                        for t in range(G):
                            for k in range(G):
                                last = te.matmul(ps_parts[:, t, :], same_b[g.s][:, k, t * P:(t + 1) * P],
                                                 parts[g.s][:, k, :, :].rearrange("p c d -> p (c d)"),
                                                 start=(k == 0), stop=(k == G - 1))
                        sig(last, "sum_ready")

                    def add_up_turned(g):
                        after("msg_moved", g.n + 1)
                        after("compared", g.n + 1)
                        after("sumT_moved", g.n)
                        for k in range(G):
                            last = te.matmul(ps_sumT, msg[:, k, :], same[g.s][:, k, :],
                                             start=(k == 0), stop=(k == G - 1))
                        sig(last, "sumT_ready")

                    def project(g, q=q):
                        after("sumT_moved", g.n + 1)
                        after("sum_moved", g.n)
                        for k in range(G):
                            last = te.matmul(ps_sum[:, k * D:(k + 1) * D], sumT[:, k * P:(k + 1) * P],
                                             wnb[q["layer"]], start=True, stop=True)
                        sig(last, "sum_ready")

                    def rel(g):
                        if behind(g, 2):
                            add_up(behind(g, 2))
                        if behind(g, 0):
                            turn_pair(g)
                            make_terms(g)

                    def pair(g):
                        if behind(g, 3):
                            add_up(behind(g, 3))
                        if behind(g, 0):
                            turn_pair(g)
                        if behind(g, 1):
                            make_terms(behind(g, 1))
                        if behind(g, 0):
                            hidden_turned(g)

                    def mlp(g):
                        if behind(g, 0):
                            turn_pair(g)
                        if behind(g, 1):
                            add_up_turned(behind(g, 1))
                        if behind(g, 0):
                            hidden(g)
                        if behind(g, 1):
                            project(behind(g, 1))

                    kind = q["kind"]
                    steps(pe, {"rel": 2, "pair": 3, "mlp": 1}[kind], {"rel": rel, "pair": pair, "mlp": mlp}[kind])


_INS = ["x", "src", "dst", "edge_attr_8", "edge_type_8", "edge_weight",
        "L0_gnn_basis1", "L0_gnn_coeff1", "L0_gnn_loop_w1", "L0_gnn_bias1",
        "L0_gnn_basis2", "L0_gnn_coeff2", "L0_gnn_loop_w2", "L0_gnn_bias2",
        "L1_gnn_pp_W", "L1_gnn_pp_b", "L1_gnn_pi_W1", "L1_gnn_pi_b1", "L1_gnn_pi_W2", "L1_gnn_ii_W", "L1_gnn_ii_b",
        "L2_gnn_We0", "L2_gnn_be0", "L2_gnn_Wn0", "L2_gnn_bn0", "L2_gnn_We1", "L2_gnn_be1", "L2_gnn_Wn1",
        "L2_gnn_bn1", "L2_gnn_We2", "L2_gnn_be2", "L2_gnn_Wn2", "L2_gnn_bn2", "L3_gnn_W"]


def kernel(**inputs):
    import numpy as np
    import concourse.bacc as bacc
    from concourse.bass_utils import run_bass_kernel_spmd as run

    nc = bacc.Bacc("TRN2", target_bir_lowering=False, num_devices=1)
    arrays, aps = {}, {}
    for name in _INS:
        v = np.ascontiguousarray(inputs[name])
        arrays["in_" + name] = v
        aps[name] = nc.dram_tensor("in_" + name, v.shape, mybir.dt.from_np(v.dtype), kind="ExternalInput").ap()
    shape = inputs["x"].shape
    out = nc.dram_tensor("out_x", shape, mybir.dt.float32, kind="ExternalOutput").ap()
    build(nc, aps, out)
    return run(nc, [arrays], core_ids=[0]).results[0]["out_x"]
```

```python
from collections import namedtuple
from contextlib import ExitStack

import concourse.bass as bass
from concourse import mybir

F32 = mybir.dt.float32
BF16 = mybir.dt.bfloat16
I32 = mybir.dt.int32
ALU = mybir.AluOpType
ACT = mybir.ActivationFunctionType
AX = mybir.AxisListType

P = 128
D = 64
G = 4
W = G * P
K = 16
R = 8
NB = 4
SLOTS = 4
EPS = 1e-5
SLOPE = 0.01
SEED = 6


Group = namedtuple("Group", "n s i odd")


def build(nc, a, out):
    N = a["x"].shape[0]
    E = a["src"].shape[0]
    Q = -(-E // (2 * W)) * 2
    T = Q * G
    PF, PR = E // T, E % T
    PAD = 1 << 20
    assert N < PAD and W >= P
    CH = P * K
    FULL = N // CH
    TAILP = (N - FULL * CH) // K
    assert FULL * CH + TAILP * K == N
    CHUNKS = FULL + (TAILP > 0)
    PAIRS = -(-CHUNKS // 2)
    TB = -(-T // P)

    ctx = ExitStack()
    with ctx:
        def sb(name, shape, dt=F32):
            return ctx.enter_context(nc.sbuf_tensor(name, shape, dt))[tuple(slice(None) for _ in shape)]

        def ps(name, shape):
            return ctx.enter_context(nc.psum_tensor(name, shape, F32))[:, :]

        def dram(name, rows, cols=D):
            return nc.dram_tensor(name, [rows, cols], F32, kind="Internal").ap()

        base1 = dram("base1", N + W)
        base2 = dram("base2", N + W)
        base3 = dram("base3", N + W)
        mlp1 = dram("mlp1", N + W)
        mlp2 = dram("mlp2", N + W)
        mlp3 = dram("mlp3", N + W)
        base4 = dram("base4", N + W)
        p1 = dram("p1", N)
        x2 = dram("x2", N)
        x3 = dram("x3", N)
        rows_dst = dram("rows_dst", T, P)
        rows_src = dram("rows_src", T, P)

        ident = sb("ident", [P, P])
        epst = sb("epst", [P, 1])
        zero = sb("zero", [P, G, D])
        loop1 = sb("loop1", [P, P])
        loop2 = sb("loop2", [P, P])
        ppw = sb("ppw", [P, P])
        wna = [sb(f"wna{l}", [P, P]) for l in range(3)]
        wnb = [sb(f"wnb{l}", [D, D]) for l in range(3)]
        we = [sb(f"we{l}", [P, D]) for l in range(3)]
        wet = [sb(f"wet{l}", [P, D]) for l in range(3)]
        bas1 = sb("bas1", [P, NB, D])
        bas2 = sb("bas2", [P, NB, D])
        w3 = sb("w3", [P, R, D])
        piw1 = sb("piw1", [P, D])
        fold = sb("fold", [D, R, D])
        pib1 = sb("pib1", [D, 1])
        names = ["L0_gnn_bias1", "L0_gnn_bias2", "L1_gnn_pp_b", "L1_gnn_ii_b",
                 "L2_gnn_be0", "L2_gnn_be1", "L2_gnn_be2", "L2_gnn_bn0", "L2_gnn_bn1", "L2_gnn_bn2"]
        bias = {n: sb("b_" + n, [P, D]) for n in names}
        iiw = sb("iiw", [D, D])
        piw2 = sb("piw2", [D, D * R])
        piw2b = sb("piw2b", [D, R, D])
        piw2t = sb("piw2t", [D, R, D])
        we_in = [sb(f"we_in{l}", [D, 2 * D + 1]) for l in range(3)]
        wet_in = sb("wet_in", [D, 3, P])
        wna_in = [sb(f"wna_in{l}", [D, 2, D]) for l in range(3)]
        wnb_in = [sb(f"wnb_in{l}", [D, 2, D]) for l in range(3)]
        cf1 = sb("cf1", [P, R, NB])
        cf2 = sb("cf2", [P, R, NB])

        key = {"dst": sb("key_dst", [P, T]), "src": sb("key_src", [P, T])}
        ends = sb("ends", [P, Q, 2, G], I32)
        target = {"dst": sb("target_dst", [P, T], I32), "src": sb("target_src", [P, T], I32)}
        gap = {"dst": sb("gap_dst", [P, T]), "src": sb("gap_src", [P, T])}
        pad = sb("pad", [P, T])
        weight = sb("weight", [P, T])
        attr = sb("attr", [P, T, R])
        coef1 = sb("coef1", [P, T, NB])
        coef2 = sb("coef2", [P, T, NB])
        coef3 = sb("coef3", [P, T, R])

        rows = [sb(f"rows{s}", [P, W]) for s in range(2)]
        rows2 = [sb(f"rows2{s}", [P, W]) for s in range(2)]
        ramp = sb("ramp", [P, W])
        gidx = [sb(f"gidx{s}", [P, 2, G], I32) for s in range(2)]
        sidx = [sb(f"sidx{s}", [P, G], I32) for s in range(2)]
        X = [sb(f"X{s}", [P, G, 2, D]) for s in range(2)]
        X1 = [x.rearrange("p k e d -> p (k e) d")[:, 0:G, :] for x in X]
        same = [sb(f"same{s}", [P, G, W]) for s in range(2)]
        cnt = [sb(f"cnt{s}", [P, 2, G]) for s in range(2)]
        same_b = [sb(f"same_b{s}", [P, G, W], BF16) for s in range(2)]
        XT = sb("XT", [P, W])
        hidT = sb("hidT", [D, W])
        hid = sb("hid", [P, G, D])
        raw = sb("raw", [P, G, D])
        rest = sb("rest", [P, G, D])
        parts = [sb(f"parts{s}", [P, G, 3, D], BF16) for s in range(2)]
        msg = sb("msg", [P, G, D])
        sumT = sb("sumT", [D, W])
        sums = [sb(f"sums{s}", [P, G, D]) for s in range(2)]
        big = [sb(f"big{s}", [P, 2 * K * D]) for s in range(2)]
        assert 5 * T <= 2 * K * D and TB * P <= 2 * K * D
        dst_in, src_in, typ_in, spare = (big[1][:, j * T:(j + 1) * T].bitcast(I32) for j in range(4))
        key_in = {"dst": dst_in, "src": src_in}
        work = big[1][:, 4 * T:5 * T]
        rowblk = big[0][:, 0:TB * P].rearrange("p (k w) -> p k w", w=P)
        terms = big[0].rearrange("p (k c) -> p k c", k=G)

        in1 = [sb(f"in1_{s}", [P, K, D]) for s in range(SLOTS)]
        in2 = [sb(f"in2_{s}", [P, K, D]) for s in range(SLOTS)]
        v = [sb(f"v{s}", [P, K, D]) for s in range(2)]
        vT = [big[s][:, 0:K * D] for s in range(2)]
        sq = [big[s][:, K * D:2 * K * D] for s in range(2)]
        o1 = [sb(f"o1_{s}", [P, K, D]) for s in range(2)] + [
            x.rearrange("p k w -> p (k w)").bitcast(F32).rearrange("p (k d) -> p k d", d=D) for x in same_b]
        o2 = [same[s // 2][:, 2 * (s % 2):2 * (s % 2) + 2, :].rearrange("p a (b d) -> p (a b) d", d=D)
              for s in range(SLOTS)]
        stat = [sb(f"stat{s}", [P, 5, K]) for s in range(SLOTS)]

        assert CHUNKS == Q // 2 and FULL == CHUNKS - 1
        HK = K // 2
        dense_x = [in1[s][:, 0:HK, :] for s in range(2)]
        dense_xT = [big[1][:, s * W:(s + 1) * W] for s in range(2)]
        dense_out = o1[0:2]
        nothing = in2[0]

        spread = ps("spread", [P, 4 * W])
        tp = [spread[:, 2 * W * s:2 * W * (s + 1)] for s in range(2)]
        mm = [ps(f"mm{s}", [P, 2 * W]) for s in range(2)]
        ps_hid = mm[0][:, 0:G * D]
        ps_hidT = mm[0][0:D, 0:W]
        ps_pair = mm[0][:, W:2 * W]
        ps_terms = {m: spread[:, 0:G * m * D].rearrange("p (h j c) -> p h j c", h=2, j=2) for m in (NB, R)}
        ps_parts = mm[1].rearrange("p (k c) -> p k c", k=G)[:, :, 0:3 * D]
        ps_sumT = tp[1][0:D, 0:W]
        ps_sum = mm[1][:, W:W + G * D]
        ps_dense_T = {"rel": mm[0][:, 0:W], "mlp": mm[1][:, 0:W]}
        ps_dense = {"rel": spread[:, 2 * W:3 * W], "mlp": spread[:, 0:W]}

        def node(src, prep, outs, mat=None, shift=None, src2=None, tanh=False):
            return dict(kind="node", src=src, src2=src2, prep=prep, mat=mat, shift=shift, tanh=tanh, outs=outs)

        def edge(kind, table, to, by="dst", **more):
            for name in ("rank", "dense", "fill"):
                more.setdefault(name, None)
            return dict(kind=kind, table=table, to=to, by=by, rows={"mlp": 0, "rel": 1, "pair": 0}[kind],
                        behind={"mlp": 3, "rel": 4, "pair": 4}[kind], **more)

        def dense(src, mat, shift, leaky):
            return dict(src=src, mat=mat, shift=shift, leaky=leaky)

        passes = [
            edge("rel", a["x"], base1, coef=coef1, mat=bas1, terms=NB, act=False, rank="dst",
                 dense=dense(a["x"], loop1, "L0_gnn_bias1", False), fill=(base2, a["x"])),
            edge("rel", base1, base2, coef=coef2, mat=bas2, terms=NB, act=True, rank="src",
                 dense=dense(base1, loop2, "L0_gnn_bias2", True)),
            node(base2, "norm", [(base3, "o1"), (p1, "o2")], ppw, "L1_gnn_pp_b", tanh=True),
            edge("pair", p1, base3, by="src", coef=attr, mat=fold, terms=R, act=False),
            node(base3, "norm", [(mlp1, "o1"), (x2, "o2")], wna[0], "L2_gnn_bn0"),
            edge("mlp", x2, mlp1, layer=0, act=False, fill=(mlp2, None)),
            edge("mlp", mlp1, mlp2, layer=1, act=True,
                 dense=dense(mlp1, wna[1], "L2_gnn_bn1", True), fill=(mlp3, None)),
            edge("mlp", mlp2, mlp3, layer=2, act=True, dense=dense(mlp2, wna[2], "L2_gnn_bn2", True)),
            node(mlp3, "leaky add norm", [(x3, "o1"), (base4, "o1")], src2=x2),
            edge("rel", x3, base4, coef=coef3, mat=w3, terms=R, act=False),
            node(base4, "norm", [(out, "o1")]),
        ]

        def sem(name):
            return ctx.enter_context(nc.semaphore(name))

        class Count:

            def __init__(self, name, start):
                self.sem, self.at, self.total = sem(name), [], start

        counts = {}

        def counted(name, start=SEED):
            counts[name] = Count(name, start)
            return counts[name]

        loaded = [counted(f"loaded{s}", 0) for s in range(SLOTS)]
        stored = [counted(f"stored{s}", 0) for s in range(SLOTS)]
        rows2_in = [counted(f"rows2_in{s}", 0) for s in range(2)]
        rows_in = [counted(f"rows_in{s}", 0) for s in range(2)]
        gidx_in = [counted(f"gidx_in{s}", 0) for s in range(2)]
        sidx_in = [counted(f"sidx_in{s}", 0) for s in range(2)]
        gathered = [counted(f"gathered{s}", 0) for s in range(2)]
        scattered = [counted(f"scattered{s}", 0) for s in range(2)]
        dense_in = [counted(f"dense_in{s}", 0) for s in range(2)]
        dense_added = counted("dense_added", 0)
        filled = counted("filled", 32)
        per_item = ["dense_turned", "dense_moved", "dense_made", "dense_done", "dense_activated", "activated", "added", "summed", "averaged", "centered", "squared", "sq_summed",
                    "rooted", "inverted", "normed", "doubled", "transposed", "moved", "multiplied", "biased",
                    "tanhed",
                    "compared", "x_used", "pair_transposed", "pair_moved", "hid_ready", "hid_moved", "terms_ready",
                    "weighted", "reduced", "msg_biased", "msg_made", "high_made", "rest_made", "mid_made",
                    "parts_made", "msg_moved", "ranked", "flagged", "gap_taken", "target_made", "edge_term", "edge_biased", "hid_summed", "sumT_ready", "sumT_moved", "sum_ready", "sum_moved"]
        c = {n: counted(n) for n in per_item}
        pool_past = sem("pool_past")
        sp_past = sem("sp_past")

        def does_mm(q):
            return q["mat"] is not None

        for q in passes:
            for x in counts.values():
                x.at.append(x.total)
            if q["kind"] == "node":
                for s in range(SLOTS):
                    n = len([i for i in range(CHUNKS) if i % SLOTS == s])
                    loaded[s].total += 16 * n * (1 + (q["src2"] is not None))
                    stored[s].total += 16 * n * len(q["outs"])
                used = {"norm": ["summed", "averaged", "centered", "squared", "sq_summed", "rooted", "inverted",
                                 "normed"],
                        "leaky add norm": ["activated", "added", "summed", "averaged", "centered", "squared",
                                           "sq_summed", "rooted", "inverted", "normed"]}[q["prep"]]
                used = used + (["transposed", "moved", "multiplied", "biased"] if does_mm(q) else [])
                used = used + (["doubled", "tanhed"] if q["tanh"] else [])
                for n in used:
                    c[n].total += CHUNKS
            else:
                ends_of = 1 if q["kind"] == "rel" else 2
                for s in range(2):
                    rows_in[s].total += 16 * (Q // 2)
                    rows2_in[s].total += 16 * (Q // 2) * (q["rank"] == "src")
                    gidx_in[s].total += 16 * (Q // 2)
                    sidx_in[s].total += 16 * (Q // 2)
                    gathered[s].total += 16 * G * ends_of * (Q // 2)
                    scattered[s].total += 16 * G * (Q // 2)
                used = ["compared", "x_used", "sum_ready", "sum_moved"] + (["activated"] if q["act"] else [])
                used += ["pair_transposed", "pair_moved"]
                if q["kind"] in ("rel", "pair"):
                    used += ["terms_ready", "weighted", "reduced", "high_made", "rest_made", "mid_made", "parts_made"]
                if q["kind"] in ("pair", "mlp"):
                    used += ["hid_ready"]
                if q["kind"] == "pair":
                    used += ["hid_moved", "msg_biased", "msg_made"]
                if q["kind"] == "mlp":
                    used += ["edge_term", "edge_biased", "hid_summed", "msg_moved", "sumT_ready", "sumT_moved"]
                used += ["ranked", "flagged", "gap_taken", "target_made"] if q["rank"] else []
                if q["dense"]:
                    used += ["dense_turned", "dense_moved", "dense_made", "dense_done"]
                    used += ["dense_activated"] if q["dense"]["leaky"] else []
                    dense_added.total += 16 * CHUNKS
                    for s in range(2):
                        dense_in[s].total += 16 * CHUNKS
                filled.total += 16 * CHUNKS * (q["fill"] is not None)
                for n in used:
                    c[n].total += Q * (2 if n in ("terms_ready", "weighted") else 1)
        spare_writes = list(zip([base1, base2, base3, mlp1, mlp2, mlp3, base4],
                                [stored[0], stored[1], stored[2], stored[3], scattered[0], scattered[1], dense_added]))
        for _, x in spare_writes:
            x.total += 16
            x.at = [n + 16 for n in x.at]

        def item(name, i, n):
            return c[name].at[i] + n

        def end_of_pass(counter, i):
            return counter.at[i + 1] if i + 1 < len(passes) else counter.total

        setup_in = sem("setup_in")
        cleared = sem("cleared")
        made = sem("made")
        step = sem("step")
        product = sem("product")
        rows_out = sem("rows_out")

        rows_made = sem("rows_made")
        weights_in = sem("weights_in")
        turned = sem("turned")
        setup_done = sem("setup_done")
        block = ctx.enter_context(nc.Block())

        setup_loads = []

        def note(dst, src):
            setup_loads.append((dst, src))

        for t, w in ((loop1, a["L0_gnn_loop_w1"]), (loop2, a["L0_gnn_loop_w2"]), (ppw, a["L1_gnn_pp_W"])):
            note(t[0:D, 0:D], w[:, :])
            note(t[D:P, D:P], w[:, :])
        for t, w in ((bas1, a["L0_gnn_basis1"]), (bas2, a["L0_gnn_basis2"]), (w3, a["L3_gnn_W"])):
            for h in range(2):
                note(t[h * D:(h + 1) * D, :, :], w.rearrange("r i o -> i r o"))
        note(pib1, a["L1_gnn_pi_b1"].unsqueeze(1))
        note(piw1[:, :], a["L1_gnn_pi_W1"][:, :])
        note(piw2[:, :], a["L1_gnn_pi_W2"][:, :])
        note(iiw[:, :], a["L1_gnn_ii_W"][:, :])
        for l in range(3):
            note(we_in[l][:, :], a[f"L2_gnn_We{l}"][:, :])
            for h in range(2):
                note(wna_in[l][:, h, :], a[f"L2_gnn_Wn{l}"][:, 0:D])
                note(wnb_in[l][:, h, :], a[f"L2_gnn_Wn{l}"][:, D:2 * D])
        for n in names:
            note(bias[n][:, :], a[n].partition_broadcast(P))
        note(cf1[:, :, :], a["L0_gnn_coeff1"].rearrange("r b -> (r b)").partition_broadcast(P))
        note(cf2[:, :, :], a["L0_gnn_coeff2"].rearrange("r b -> (r b)").partition_broadcast(P))
        for t, s in ((key_in["dst"], a["dst"]), (key_in["src"], a["src"]), (typ_in, a["edge_type_8"]),
                     (weight, a["edge_weight"])):
            note(t[0:PF, :], s[0:PF * T].rearrange("(p t) -> p t", t=T))
            if PR:
                note(t[PF:PF + 1, 0:PR], s[PF * T:E].unsqueeze(0))
        note(attr[0:PF, :, :], a["edge_attr_8"][0:PF * T, :].rearrange("(p t) b -> p t b", t=T))
        if PR:
            note(attr[PF:PF + 1, 0:PR, :], a["edge_attr_8"][PF * T:E, :].unsqueeze(0))

        def chunk_rows(t, at, parts):
            if isinstance(at, int):
                return t[at * CH:at * CH + parts * K, :].rearrange("(p k) d -> p k d", k=K)
            return t[bass.ds(at * CH, CH), :].rearrange("(p k) d -> p k d", k=K)

        def behind(g, lag, count=Q):
            s = (g.s - lag) % 2
            back = (lag - g.s + s) // 2
            at = Group(g.n - lag, s, g.i - back, (g.odd + back) % 2)
            return None if isinstance(at.n, int) and not 0 <= at.n < count else at

        def steps(eng, lag, do, count=Q, alike=2 * FULL, body=2):
            peel = -(-lag // body) * body
            loops = (alike - peel) // body
            for n in range(peel):
                do(Group(n, n % 2, n // 2, n // 2 % 2))
            with eng.Fori(0, loops) as i:
                for s in range(body):
                    do(Group(i * body + peel + s, s % 2, i * (body // 2) + (peel + s) // 2, (peel + s) // 2 % 2))
            for n in range(peel + body * loops, count + lag):
                do(Group(n, n % 2, n // 2, n // 2 % 2))

        def pairs(eng, lag, do):
            steps(eng, lag, do, PAIRS, FULL // 2)

        def before(g, lag=0):
            g = behind(g, lag, PAIRS)
            if g is None:
                return []
            out = [(g.n * 2 + h, 2 * g.s + h, P, g.i) for h in range(2)]
            if isinstance(g.n, int):
                out = [(ch, s, P if ch < FULL else TAILP, i) for ch, s, _, i in out if ch < CHUNKS]
            return out

        def part_of(h):
            return TAILP if isinstance(h.i, int) and h.i == FULL else P

        def bc_d(t):
            return t.unsqueeze(2).to_broadcast([P, t.shape[1], D])

        def bc_k(t, k):
            return t.unsqueeze(1).to_broadcast([P, k, D])

        @block.sync
        def _(sp):
            sp.wait_ge(cleared, 1)
            for dst, src in setup_loads:
                sp.dma_start(dst, src).then_inc(setup_in, 16)
            n = 0
            for j, name in enumerate(("dst", "src")):
                sp.wait_ge(rows_made, j + 1)
                for k in range(TB):
                    m = min(P, T - k * P)
                    sp.dma_start((rows_dst, rows_src)[j][k * P:k * P + m, :], rowblk[0:m, k, :]).then_inc(rows_out, 16)
                    n += 16
                sp.wait_ge(rows_out, n)
            for n, q in enumerate(passes):
                if n:
                    for s in range(2):
                        sp.wait_ge(scattered[s].sem, scattered[s].at[n])
                    sp.wait_ge(dense_added.sem, dense_added.at[n])
                if q["kind"] == "node":
                    def load(g, q=q, n=n):
                        for ch, s, parts, _ in before(g):
                            sp.wait_ge(c["normed"].sem, item("normed", n, ch - SLOTS + 1))
                            sp.dma_start(in1[s][0:parts, :, :], chunk_rows(q["src"], ch, parts)
                                         ).then_inc(loaded[s].sem, 16)
                            if q["src2"] is not None:
                                sp.dma_start(in2[s][0:parts, :, :], chunk_rows(q["src2"], ch, parts)
                                             ).then_inc(loaded[s].sem, 16)

                    pairs(sp, 0, load)
                else:
                    table = rows_dst if q["by"] == "dst" else rows_src
                    tgt = target[q["by"]]
                    if q["by"] == "src":
                        sp.wait_ge(c["target_made"].sem, c["target_made"].at[n])

                    def load(g, q=q, n=n, table=table, tgt=tgt):
                        now, at, old = behind(g, 0), behind(g, q["rows"]), behind(g, q["behind"])
                        if now:
                            sp.wait_ge(c["x_used"].sem, item("x_used", n, now.n - 1))
                            sp.dma_start(gidx[now.s], ends[:, bass.ds(now.n, 1), :, :].rearrange("p a e t -> p (a e) t")
                                         ).then_inc(gidx_in[now.s].sem, 16)
                        if old:
                            if q["rank"] == "dst":
                                sp.wait_ge(c["target_made"].sem, item("target_made", n, old.n + 1))
                                sp.sem_inc(sp_past, 1)
                            sp.wait_ge(scattered[old.s].sem, scattered[old.s].at[n] + 16 * G * old.i)
                            sp.dma_start(sidx[old.s], tgt[:, bass.ds(old.n * G, G)]).then_inc(sidx_in[old.s].sem, 16)
                        if at:
                            sp.wait_ge(c["compared"].sem, item("compared", n, at.n - 1))
                            if q["rank"]:
                                sp.wait_ge(c["ranked"].sem, item("ranked", n, at.n - 1))
                            sp.dma_start(rows[at.s], table[bass.ds(at.n * G, G), :]
                                         .rearrange("t p -> (t p)").partition_broadcast(P)).then_inc(rows_in[at.s].sem, 16)
                            if q["rank"] == "src":
                                sp.dma_start(rows2[at.s], rows_src[bass.ds(at.n * G, G), :]
                                             .rearrange("t p -> (t p)").partition_broadcast(P)
                                             ).then_inc(rows2_in[at.s].sem, 16)
                        half = behind(g, 1)
                        if q["dense"] and half:
                            sp.wait_ge(c["dense_turned"].sem, item("dense_turned", n, half.n - 1))
                            m = part_of(half)
                            sp.dma_start(dense_x[half.s][0:m, :, :],
                                         chunk_rows(q["dense"]["src"], half.i, m)[:, half.s * HK:(half.s + 1) * HK, :]
                                         ).then_inc(dense_in[half.s].sem, 16)

                    steps(sp, q["behind"], load)

        @block.gpsimd
        def _(pool):
            nc.gpsimd.memset(ident[:, :], 0.0).then_inc(made, 1)
            nc.gpsimd.memset(ramp[:, :], 1.0).then_inc(made, 1)
            nc.gpsimd.memset(epst[:, :], EPS).then_inc(made, 1)
            nc.gpsimd.memset(zero[:, :, :], 0.0).then_inc(made, 1)
            pool.sem_inc(c["normed"].sem, SEED)
            pool.wait_ge(made, 4)
            nc.gpsimd.affine_select(out=ident[:, :], in_=ident[:, :], compare_op=ALU.not_equal, fill=1.0, base=0,
                                    pattern=[[-1, P]], channel_multiplier=1).then_inc(made, 1)
            nc.gpsimd.affine_select(out=ramp, in_=ramp, compare_op=ALU.is_gt, fill=0.0, base=W - P,
                                    pattern=[[-1, W]], channel_multiplier=1).then_inc(made, 1)
            nc.gpsimd.iota(spare, pattern=[[0, Q], [P, G]], base=N, channel_multiplier=1).then_inc(made, 1)
            for t, x in spare_writes:
                pool.dma_start(t[N:N + W, :].rearrange("(p k) d -> p k d", k=G), zero[:, :, :]).then_inc(x.sem, 16)

            for n, q in enumerate(passes):
                if q["kind"] == "node":
                    ready = {"o1": "normed" if not does_mm(q) else "doubled" if q["tanh"] else
                             "biased",
                             "o2": "tanhed" if q["tanh"] else "normed"}
                    buf = {"o1": o1, "o2": o2}

                    def norm_and_store(g, q=q, n=n, ready=ready, buf=buf):
                        for ch, s, _, i in before(g):
                            pool.wait_ge(c["inverted"].sem, item("inverted", n, ch + 1))
                            pool.sem_inc(pool_past, 1)
                            if q["tanh"]:
                                to = v[s % 2]
                                pool.wait_ge(c["transposed"].sem, item("transposed", n, ch - 1))
                                pool.sem_inc(pool_past, 1)
                                pool.wait_ge(c["doubled"].sem, item("doubled", n, ch - 1))
                                pool.sem_inc(pool_past, 1)
                            else:
                                to = o2[s] if does_mm(q) else o1[s]
                                pool.wait_ge(stored[s].sem, stored[s].at[n] + 16 * len(q["outs"]) * i)
                                pool.sem_inc(pool_past, 1)
                            nc.gpsimd.tensor_tensor(to[:, :, :], in1[s][:, :, :], bc_d(stat[s][:, 4, :]), ALU.mult
                                                    ).then_inc(c["normed"].sem, 1)
                        for ch, s, parts, _ in before(g, 1):
                            for t, o in q["outs"]:
                                pool.wait_ge(c[ready[o]].sem, item(ready[o], n, ch + 1))
                                pool.sem_inc(pool_past, 1)
                                pool.dma_start(chunk_rows(t, ch, parts), buf[o][s][0:parts, :, :]
                                               ).then_inc(stored[s].sem, 16)

                    pairs(pool, 1, norm_and_store)
                else:
                    for s in range(SLOTS):
                        pool.wait_ge(stored[s].sem, stored[s].at[n])
                    if n:
                        for s in range(2):
                            pool.wait_ge(scattered[s].sem, scattered[s].at[n])
                        pool.wait_ge(dense_added.sem, dense_added.at[n])
                    if q["dense"]:
                        pool.wait_ge(filled.sem, filled.at[n])
                    ends_of = 1 if q["kind"] == "rel" else 2

                    def gather(g, part, q=q, n=n, ends_of=ends_of):
                        if part == 0:
                            pool.wait_ge(c["x_used"].sem, item("x_used", n, g.n - 1))
                            pool.sem_inc(pool_past, 1)
                            pool.wait_ge(gidx_in[g.s].sem, gidx_in[g.s].at[n] + 16 * (g.i + 1))
                            pool.sem_inc(pool_past, 1)
                        for j in range(G * ends_of // 2):
                            k, e = divmod(part * G * ends_of // 2 + j, ends_of)
                            pool.indirect_dma_start(
                                out=X[g.s][:, k, e, :] if ends_of == 2 else X1[g.s][:, k, :], out_offset=None,
                                in_=q["table"][0:N, :],
                                in_offset=bass.IndirectOffsetOnAxis(ap=gidx[g.s][:, e, k:k + 1], axis=0),
                            ).then_inc(gathered[g.s].sem, 16)

                    def add_dense(g, q=q, n=n):
                        pool.wait_ge(c["dense_done"].sem, item("dense_done", n, 2 * g.i + 2))
                        pool.sem_inc(pool_past, 1)
                        last = behind(g, q["behind"] - 3)
                        pool.wait_ge(scattered[last.s].sem, scattered[last.s].at[n] + 16 * G * (last.i + 1))
                        pool.sem_inc(pool_past, 1)
                        m = part_of(g)
                        pool.dma_start(chunk_rows(q["to"], g.i, m), dense_out[g.odd][0:m, :, :], accum_op=ALU.add
                                       ).then_inc(dense_added.sem, 16)

                    def scatter(g, q=q, n=n):
                        pool.wait_ge(c["sum_moved"].sem, item("sum_moved", n, g.n + 1))
                        pool.sem_inc(pool_past, 1)
                        pool.wait_ge(sidx_in[g.s].sem, sidx_in[g.s].at[n] + 16 * (g.i + 1))
                        pool.sem_inc(pool_past, 1)
                        pool.wait_ge(scattered[1 - g.s].sem, scattered[1 - g.s].at[n] + 16 * G * (g.i + g.s))
                        pool.sem_inc(pool_past, 1)
                        if q["dense"]:
                            chunks = g.i + (g.s + q["behind"] - 3) // 2
                            pool.wait_ge(dense_added.sem, dense_added.at[n] + 16 * chunks)
                            pool.sem_inc(pool_past, 1)
                        for k in range(G):
                            pool.indirect_dma_start(
                                out=q["to"], out_offset=bass.IndirectOffsetOnAxis(ap=sidx[g.s][:, k:k + 1], axis=0),
                                in_=sums[g.s][:, k, :], in_offset=None, compute_op=ALU.add,
                            ).then_inc(scattered[g.s].sem, 16)

                    def fetch_and_add(g, q=q):
                        if behind(g, 0):
                            gather(g, 0)
                        if q["dense"] and g.s and behind(g, 4):
                            add_dense(behind(g, 4))
                        if behind(g, 0):
                            gather(g, 1)
                        if behind(g, q["behind"]):
                            scatter(behind(g, q["behind"]))

                    steps(pool, 4 if q["dense"] else q["behind"], fetch_and_add, body=4 if q["dense"] else 2)
            for s in range(SLOTS):
                pool.wait_ge(stored[s].sem, stored[s].total)

        by_dve = ["dense_done", "dense_activated", "activated", "added", "summed", "averaged", "centered", "sq_summed", "inverted",
                  "biased", "compared", "weighted", "reduced", "msg_biased", "rest_made", "parts_made",
                  "msg_moved", "edge_term", "edge_biased", "hid_summed", "ranked", "flagged", "gap_taken", "target_made"]
        by_act = ["dense_moved", "squared", "rooted", "doubled", "moved", "tanhed", "pair_moved", "hid_moved", "msg_made",
                  "high_made", "mid_made", "sumT_moved", "sum_moved"]
        by_pe = ["dense_turned", "dense_made", "transposed", "multiplied", "pair_transposed", "hid_ready", "terms_ready", "sumT_ready",
                 "sum_ready", "x_used"]

        @block.vector
        def _(dve):
            vec = nc.vector
            for name in by_dve:
                dve.sem_inc(c[name].sem, SEED)
            done = [0]

            def link(ins):
                done[0] += 1
                ins.then_inc(step, 1)
                dve.wait_ge(step, done[0])

            for t in [loop1, loop2, ppw, *wna, weight, *sums, *X, *in1, *in2]:
                link(vec.memset(t[:], 0.0))
            link(vec.memset(attr[:, :, :], 0.0))
            for t in (*key_in.values(), typ_in):
                link(vec.memset(t[:, :], PAD))
            dve.sem_inc(cleared, 1)
            dve.wait_ge(setup_in, 16 * len(setup_loads))
            dve.wait_ge(made, 7)
            for e, name in enumerate(("src", "dst")):
                link(vec.tensor_copy(key[name][:, :], key_in[name][:, :]))
                link(vec.scalar_tensor_tensor(out=ends[:, :, e, :], in0=key[name].rearrange("p (q t) -> p q t", t=G),
                                              scalar=float(N), in1=key[name].rearrange("p (q t) -> p q t", t=G),
                                              op0=ALU.is_lt, op1=ALU.mult))
                link(vec.tensor_tensor(gap[name], spare, key[name], ALU.subtract))
            link(vec.tensor_scalar(pad, key["dst"], float(N), None, ALU.is_ge))
            link(vec.tensor_copy(work[:, :], typ_in[:, :]))
            for r in range(R):
                link(vec.tensor_scalar(coef3[:, :, r], work[:, :], float(r), None, ALU.is_equal))
            for cf, coef in ((cf1, coef1), (cf2, coef2)):
                for b in range(NB):
                    link(vec.tensor_scalar(coef[:, :, b], coef3[:, :, 0], cf[:, 0, b:b + 1], None, ALU.mult))
                    for r in range(1, R):
                        link(vec.scalar_tensor_tensor(out=coef[:, :, b], in0=coef3[:, :, r], scalar=cf[:, r, b:b + 1],
                                                      in1=coef[:, :, b], op0=ALU.mult, op1=ALU.add))
            link(vec.tensor_tensor(coef3[:, :, :], coef3[:, :, :], weight.unsqueeze(2).to_broadcast([P, T, R]),
                                   ALU.mult))
            for b in range(R):
                link(vec.tensor_copy(piw2b[:, b, :], piw2.rearrange("f (c b) -> f c b", b=R)[:, :, b]))
            for l in range(3):
                link(vec.tensor_copy(wet_in[:, l, :], we_in[l][:, 2 * D:2 * D + 1].to_broadcast([D, P])))
            dve.sem_inc(weights_in, 1)
            dve.wait_ge(product, 1)
            for l in range(3):
                link(vec.tensor_copy(we[l][:, :], tp[0][:, l * D:(l + 1) * D]))
                link(vec.tensor_copy(wet[l][:, :], tp[0][:, (3 + l) * D:(4 + l) * D]))
            dve.wait_ge(product, 2)
            for l in range(3):
                link(vec.tensor_copy(wna[l][0:D, 0:D], tp[1][0:D, l * D:(l + 1) * D]))
                link(vec.tensor_copy(wna[l][D:P, D:P], tp[1][D:P, l * D:(l + 1) * D]))
                link(vec.tensor_copy(wnb[l][:, :], tp[1][0:D, (3 + l) * D:(4 + l) * D]))
            dve.wait_ge(product, 3)
            link(vec.tensor_copy(piw2t[:, :, :].rearrange("p b d -> p (b d)"), mm[0][0:D, 0:W]))
            dve.sem_inc(turned, 1)
            dve.wait_ge(product, 4)
            link(vec.tensor_copy(fold.rearrange("p b d -> p (b d)"), mm[1][0:D, 0:R * D]))
            for j, name in enumerate(("dst", "src")):
                dve.wait_ge(product, 5 + j)
                if j:
                    dve.wait_ge(rows_out, 16 * TB)
                for k in range(TB):
                    m = min(P, T - k * P)
                    link(vec.tensor_copy(rowblk[0:m, k, :], tp[j][0:m, k * P:(k + 1) * P]))
                dve.sem_inc(rows_made, 1)
            dve.sem_inc(setup_done, 1)

            for n, q in enumerate(passes):
                def after(name, cnt_, n=n):
                    dve.wait_ge(c[name].sem, item(name, n, cnt_))

                def sig(ins, name):
                    ins.then_inc(c[name].sem, 1)

                if q["kind"] == "node":
                    if n:
                        for s in range(2):
                            dve.wait_ge(scattered[s].sem, scattered[s].at[n])
                        dve.wait_ge(dense_added.sem, dense_added.at[n])
                    prep = q["prep"]
                    n_in = 1 + (q["src2"] is not None)

                    def chunks(g, q=q, n=n, prep=prep, n_in=n_in):
                        group = before(g)

                        def arrived(s, i):
                            dve.wait_ge(loaded[s].sem, loaded[s].at[n] + 16 * n_in * (i + 1))

                        def free(s, i):
                            dve.wait_ge(stored[s].sem, stored[s].at[n] + 16 * len(q["outs"]) * i)

                        if prep == "leaky add norm":
                            for ch, s, _, i in group:
                                arrived(s, i)
                                sig(vec.scalar_tensor_tensor(out=v[s % 2][:, :, :], in0=in1[s][:, :, :], scalar=SLOPE,
                                                             in1=in1[s][:, :, :], op0=ALU.mult, op1=ALU.max),
                                    "activated")
                            for ch, s, _, i in group:
                                after("activated", ch + 1)
                                sig(vec.tensor_tensor(in1[s][:, :, :], v[s % 2][:, :, :], in2[s][:, :, :], ALU.add),
                                    "added")
                        if "norm" in prep:
                            for ch, s, _, i in group:
                                if prep == "norm":
                                    arrived(s, i)
                                else:
                                    after("added", ch + 1)
                                sig(vec.tensor_reduce(stat[s][:, 0, :], in1[s][:, :, :], AX.X, ALU.add), "summed")
                            for ch, s, _, i in group:
                                after("summed", ch + 1)
                                sig(vec.tensor_scalar(stat[s][:, 1, :], stat[s][:, 0, :], -1.0 / D, None, ALU.mult),
                                    "averaged")
                            for ch, s, _, i in group:
                                after("averaged", ch + 1)
                                sig(vec.tensor_tensor(in1[s][:, :, :], in1[s][:, :, :], bc_d(stat[s][:, 1, :]),
                                                      ALU.add), "centered")
                            for ch, s, _, i in group:
                                after("squared", ch + 1)
                                sig(vec.tensor_reduce(stat[s][:, 2, :],
                                                      sq[s % 2].rearrange("p (k d) -> p k d", d=D), AX.X, ALU.add),
                                    "sq_summed")
                        if does_mm(q):
                            for ch, s, _, i in before(g, 1):
                                after("multiplied", ch + 1)
                                free(s, i)
                                to = o2[s] if q["tanh"] else o1[s]
                                sig(vec.tensor_tensor(to[:, :, :],
                                                      mm[s % 2].rearrange("p (k d) -> p k d", d=D),
                                                      bc_k(bias[q["shift"]][:, :], K), ALU.add), "biased")
                        if "norm" in prep:
                            for ch, s, _, i in group:
                                after("rooted", ch + 1)
                                sig(vec.reciprocal(stat[s][:, 4, :], stat[s][:, 3, :]), "inverted")

                    pairs(dve, 1 if does_mm(q) else 0, chunks)
                else:
                    for s in range(SLOTS):
                        dve.wait_ge(stored[s].sem, stored[s].at[n])
                    ends_of = 1 if q["kind"] == "rel" else 2
                    tok = key[q["by"]]
                    matrix = same if q["kind"] == "mlp" else same_b

                    def compare(g, tok=tok, q=q, matrix=matrix):
                        dve.wait_ge(rows_in[g.s].sem, rows_in[g.s].at[n] + 16 * (g.i + 1))
                        after("sumT_ready" if q["kind"] == "mlp" else "sum_ready", g.n - 1)
                        for k in range(G):
                            last = vec.tensor_scalar(matrix[g.s][:, k, :], rows[g.s],
                                                     tok[:, bass.ds(g.n * G + k, 1)], None, ALU.is_equal)
                        sig(last, "compared")

                    def activate(g, q=q, ends_of=ends_of):
                        if q["act"]:
                            dve.wait_ge(gathered[g.s].sem, gathered[g.s].at[n] + 16 * G * ends_of * (g.i + 1))
                            x = X[g.s] if ends_of == 2 else X1[g.s]
                            sig(vec.scalar_tensor_tensor(out=x, in0=x, scalar=SLOPE, in1=x, op0=ALU.mult, op1=ALU.max),
                                "activated")

                    def rank(g, q=q):
                        name = q["rank"]
                        if name == "src":
                            dve.wait_ge(rows2_in[g.s].sem, rows2_in[g.s].at[n] + 16 * (g.i + 1))
                        row = rows[g.s] if name == "dst" else rows2[g.s]
                        for k in range(G):
                            m = (k + 1) * P
                            last = vec.scalar_tensor_tensor(
                                out=same[g.s][:, k, 0:m], in0=row[:, 0:m], scalar=key[name][:, bass.ds(g.n * G + k, 1)],
                                in1=ramp[:, W - m:W], op0=ALU.is_equal, op1=ALU.mult,
                                accum_out=cnt[g.s][:, 0, k:k + 1])
                        sig(last, "ranked")

                    def flag(g, q=q):
                        name, at = q["rank"], bass.ds(g.n * G, G)
                        after("ranked", g.n + 1)
                        sig(vec.scalar_tensor_tensor(out=cnt[g.s][:, 0, :], in0=cnt[g.s][:, 0, :], scalar=0.5,
                                                     in1=pad[:, at], op0=ALU.is_gt, op1=ALU.max), "flagged")

                    def take_gap(g, q=q):
                        name, at = q["rank"], bass.ds(g.n * G, G)
                        after("flagged", g.n + 1)
                        sig(vec.tensor_tensor(cnt[g.s][:, 1, :], cnt[g.s][:, 0, :], gap[name][:, at], ALU.mult),
                            "gap_taken")

                    def make_target(g, q=q):
                        name, at = q["rank"], bass.ds(g.n * G, G)
                        after("gap_taken", g.n + 1)
                        sig(vec.tensor_tensor(target[name][:, at], cnt[g.s][:, 1, :], key[name][:, at], ALU.add),
                            "target_made")

                    def weigh(g, q=q):
                        m = q["terms"]
                        after("reduced", g.n)
                        for h in range(2):
                            after("terms_ready", 2 * g.n + h + 1)
                            cf = q["coef"][:, bass.ds(g.n * G, G), :].rearrange("p (j h) r -> p h j r", h=2)[:, h, :, :]
                            cf = cf.unsqueeze(3).to_broadcast([P, 2, m, D])
                            sig(vec.tensor_tensor(
                                terms.rearrange("p (j h) c -> p h j c", h=2)[:, h, :, 0:m * D]
                                .rearrange("p j (r d) -> p j r d", d=D),
                                ps_terms[m][:, h, :, :].rearrange("p j (r d) -> p j r d", d=D), cf, ALU.mult),
                                "weighted")

                    def reduce(g, q=q):
                        m = q["terms"]
                        after("weighted", 2 * g.n + 2)
                        after("rest_made", g.n)
                        if q["kind"] == "pair":
                            after("msg_biased", g.n)
                        sig(vec.tensor_reduce(raw, terms[:, :, 0:m * D].rearrange("p k (r d) -> p k d r", d=D),
                                              AX.X, ALU.add), "reduced")
                        if q["kind"] == "pair":
                            after("reduced", g.n + 1)
                            after("msg_made", g.n)
                            sig(vec.tensor_tensor(hid, raw, bc_k(bias["L1_gnn_ii_b"], G), ALU.add), "msg_biased")

                    def part_rest(g, q=q):
                        m = msg if q["kind"] == "pair" else raw
                        after("high_made", g.n + 1)
                        after("parts_made", g.n)
                        sig(vec.tensor_tensor(rest, m, parts[g.s][:, :, 0, :], ALU.subtract), "rest_made")

                    def part_low(g):
                        after("mid_made", g.n + 1)
                        sig(vec.tensor_tensor(parts[g.s][:, :, 2, :], rest, parts[g.s][:, :, 1, :], ALU.subtract),
                            "parts_made")

                    def join_sums(g):
                        after("sum_ready", g.n + 1)
                        dve.wait_ge(scattered[g.s].sem, scattered[g.s].at[n] + 16 * G * g.i)
                        sig(vec.tensor_reduce(sums[g.s], ps_parts.rearrange("p k (c d) -> p k d c", d=D), AX.X,
                                              ALU.add), "sum_moved")

                    def dense_leaky(h):
                        dve.wait_ge(dense_in[h.s].sem, dense_in[h.s].at[n] + 16 * (h.i + 1))
                        x = dense_x[h.s]
                        sig(vec.scalar_tensor_tensor(out=x, in0=x, scalar=SLOPE, in1=x, op0=ALU.mult, op1=ALU.max),
                            "dense_activated")

                    def dense_finish(h, q=q):
                        after("dense_made", h.n + 1)
                        if not (isinstance(h.i, int) and h.i == 0):
                            dve.wait_ge(dense_added.sem, dense_added.at[n] + 16 * (h.i - 1))
                        sig(vec.tensor_tensor(dense_out[h.odd][:, h.s * HK:(h.s + 1) * HK, :],
                                              ps_dense[kind].rearrange("p (k d) -> p k d", d=D),
                                              bc_k(bias[q["dense"]["shift"]], HK), ALU.add), "dense_done")

                    def finish(g, q=q):
                        if q["dense"] and behind(g, 3):
                            dense_finish(behind(g, 3))

                    def both(g, q=q):
                        do[kind](g)
                        if q["dense"] and q["dense"]["leaky"] and behind(g, 1):
                            dense_leaky(behind(g, 1))

                    def rel(g, q=q):
                        if behind(g, 2):
                            part_rest(behind(g, 2))
                        if behind(g, 0):
                            activate(g)
                        if behind(g, 2):
                            compare(behind(g, 2))
                        ranked = q["rank"] and behind(g, 2)
                        if ranked:
                            rank(ranked)
                        if behind(g, 2):
                            part_low(behind(g, 2))
                        if ranked:
                            flag(ranked)
                        finish(g)
                        if ranked:
                            take_gap(ranked)
                        if behind(g, 1):
                            weigh(behind(g, 1))
                        if ranked:
                            make_target(ranked)
                        if behind(g, 1):
                            reduce(behind(g, 1))
                        if behind(g, 3):
                            join_sums(behind(g, 3))

                    def pair(g):
                        if behind(g, 2):
                            part_rest(behind(g, 2))
                        if behind(g, 3):
                            join_sums(behind(g, 3))
                        if behind(g, 1):
                            compare(behind(g, 1))
                        if behind(g, 2):
                            part_low(behind(g, 2))
                        if behind(g, 1):
                            weigh(behind(g, 1))
                            reduce(behind(g, 1))

                    def mlp(g, q=q):
                        if not behind(g, 0):
                            finish(g)
                            return
                        activate(g)
                        compare(g)
                        after("msg_moved", g.n)
                        sig(vec.tensor_tensor(hid, bc_k(wet[q["layer"]], G), bc_d(weight[:, bass.ds(g.n * G, G)]),
                                              ALU.mult), "edge_term")
                        after("edge_term", g.n + 1)
                        sig(vec.tensor_tensor(hid, hid, bc_k(bias[f"L2_gnn_be{q['layer']}"], G), ALU.add),
                            "edge_biased")
                        finish(g)
                        after("hid_ready", g.n + 1)
                        after("edge_biased", g.n + 1)
                        sig(vec.tensor_tensor(hid, hid, ps_hid.rearrange("p (k d) -> p k d", d=D), ALU.add),
                            "hid_summed")
                        after("hid_summed", g.n + 1)
                        after("sumT_ready", g.n)
                        sig(vec.scalar_tensor_tensor(out=msg, in0=hid, scalar=SLOPE, in1=hid, op0=ALU.mult,
                                                     op1=ALU.max), "msg_moved")

                    kind, do = q["kind"], {"rel": rel, "pair": pair, "mlp": mlp}
                    steps(dve, 3 if q["dense"] or kind != "mlp" else 0, both, body=4 if q["dense"] else 2)

        @block.scalar
        def _(act):
            sc = nc.scalar
            for name in by_act:
                act.sem_inc(c[name].sem, SEED)
            act.wait_ge(cleared, 1)
            act.wait_ge(setup_in, 16 * len(setup_loads))
            act.dma_start(base1[0:FULL * CH, :].rearrange("(c p k) d -> p c (k d)", p=P, k=K),
                          nothing.rearrange("p k d -> p (k d)").unsqueeze(1).to_broadcast([P, FULL, K * D])
                          ).then_inc(filled.sem, 16)
            act.dma_start(chunk_rows(base1, FULL, TAILP), nothing[0:TAILP, :, :]).then_inc(filled.sem, 16)
            act.wait_ge(setup_done, 1)
            for n, q in enumerate(passes):
                def after(name, cnt_, n=n):
                    act.wait_ge(c[name].sem, item(name, n, cnt_))

                def sig(ins, name):
                    ins.then_inc(c[name].sem, 1)

                if q["kind"] == "node":
                    def chunks(g, q=q, n=n):
                        if "norm" in q["prep"]:
                            for ch, s, _, i in before(g):
                                after("centered", ch + 1)
                                after("sq_summed", ch - 1)
                                sig(sc.activation(sq[s % 2].rearrange("p (k d) -> p k d", d=D), in1[s], ACT.Square),
                                    "squared")
                            for ch, s, _, i in before(g):
                                after("sq_summed", ch + 1)
                                sig(sc.activation(stat[s][:, 3, :], stat[s][:, 2, :], ACT.Sqrt, bias=epst,
                                                  scale=1.0 / D), "rooted")
                        if q["tanh"]:
                            for ch, s, _, i in before(g, 1):
                                after("biased", ch + 1)
                                sig(sc.activation(o2[s], o2[s], ACT.Tanh), "tanhed")
                            for ch, s, _, i in before(g):
                                after("normed", ch + 1)
                                act.wait_ge(stored[s].sem, stored[s].at[n] + 32 * i)
                                sig(sc.mul(o1[s], v[s % 2], 2.0), "doubled")
                        if does_mm(q):
                            for ch, s, _, i in before(g):
                                after("transposed", ch + 1)
                                after("multiplied", ch - 1)
                                sig(sc.copy(vT[s % 2], tp[s % 2]), "moved")

                    pairs(act, 1 if q["tanh"] else 0, chunks)
                else:
                    def move_pair(g, q=q):
                        after("pair_transposed", g.n + 1)
                        if q["kind"] == "rel":
                            after("terms_ready", 2 * g.n)
                        else:
                            after("hid_ready", g.n)
                        cols = W // 2 if q["kind"] == "rel" else W
                        sig(sc.copy(XT[:, 0:cols], ps_pair[:, 0:cols]), "pair_moved")

                    def move_hidden(g):
                        after("hid_ready", g.n + 1)
                        after("terms_ready", 2 * g.n)
                        sig(sc.activation(hidT, ps_hidT, ACT.Identity, bias=pib1), "hid_moved")

                    def part_high(g, q=q):
                        if q["kind"] == "pair":
                            after("msg_biased", g.n + 1)
                            after("rest_made", g.n)
                            sig(sc.activation(msg, hid, ACT.Tanh), "msg_made")
                            after("msg_made", g.n + 1)
                        else:
                            after("reduced", g.n + 1)
                        after("sum_ready", g.n - 1)
                        sig(sc.copy(parts[g.s][:, :, 0, :], msg if q["kind"] == "pair" else raw), "high_made")

                    def part_mid(g):
                        after("rest_made", g.n + 1)
                        sig(sc.copy(parts[g.s][:, :, 1, :], rest), "mid_made")

                    def move_sums(g):
                        after("sum_ready", g.n + 1)
                        act.wait_ge(scattered[g.s].sem, scattered[g.s].at[n] + 16 * G * g.i)
                        sig(sc.copy(sums[g.s].rearrange("p k d -> p (k d)"), ps_sum), "sum_moved")

                    def rel(g):
                        if behind(g, 2):
                            part_high(behind(g, 2))
                            part_mid(behind(g, 2))
                        if behind(g, 0):
                            move_pair(g)
                        if q["dense"] and behind(g, 2):
                            dense_move(behind(g, 2))

                    def pair(g):
                        if behind(g, 2):
                            part_high(behind(g, 2))
                        if behind(g, 0):
                            move_pair(g)
                        if behind(g, 2):
                            part_mid(behind(g, 2))
                        if behind(g, 0):
                            move_hidden(g)

                    def mlp(g):
                        if behind(g, 0):
                            move_pair(g)
                        if q["dense"] and behind(g, 2):
                            dense_move(behind(g, 2))
                        old = behind(g, 1)
                        if old:
                            after("sumT_ready", old.n + 1)
                            after("sum_ready", old.n)
                            sig(sc.copy(sumT, ps_sumT), "sumT_moved")
                            move_sums(old)

                    def dense_move(h):
                        after("dense_turned", h.n + 1)
                        after("dense_made", h.n - 1)
                        sig(sc.copy(dense_xT[h.s], ps_dense_T[kind]), "dense_moved")

                    def both(g, q=q):
                        do[kind](g)
                        if q["fill"] and g.s == 0 and behind(g, 0):
                            to, rows_of = q["fill"]
                            m = part_of(g)
                            act.dma_start(chunk_rows(to, g.i, m), nothing[0:m, :, :] if rows_of is None else
                                          chunk_rows(rows_of, g.i, m)).then_inc(filled.sem, 16)

                    kind, do = q["kind"], {"rel": rel, "pair": pair, "mlp": mlp}
                    steps(act, 1 if kind == "mlp" and not q["dense"] else 2, both)

        @block.tensor
        def _(pe):
            te = nc.tensor
            for name in by_pe:
                pe.sem_inc(c[name].sem, SEED)
            pe.wait_ge(weights_in, 1)
            for l in range(3):
                te.transpose(tp[0][:, l * D:(l + 1) * D], we_in[l][:, 0:2 * D], ident[0:D, 0:D])
            for l in range(3):
                last = te.matmul(tp[0][:, (3 + l) * D:(4 + l) * D], wet_in[:, l, :], ident[0:D, 0:D],
                                 start=True, stop=True)
            last.then_inc(product, 1)
            for l in range(3):
                te.transpose(tp[1][:, l * D:(l + 1) * D], wna_in[l][:, :, :].rearrange("p h d -> p (h d)"),
                             ident[0:D, 0:D])
            for l in range(3):
                last = te.transpose(tp[1][:, (3 + l) * D:(4 + l) * D],
                                    wnb_in[l][:, :, :].rearrange("p h d -> p (h d)"), ident[0:D, 0:D])
            last.then_inc(product, 1)
            for b in range(R):
                last = te.transpose(mm[0][0:D, b * D:(b + 1) * D], piw2b[:, b, :], ident[0:D, 0:D])
            last.then_inc(product, 1)
            pe.wait_ge(turned, 1)
            for b in range(R):
                last = te.matmul(mm[1][0:D, b * D:(b + 1) * D], piw2t[:, b, :], iiw, start=True, stop=True)
            last.then_inc(product, 1)
            for j, name in enumerate(("dst", "src")):
                for k in range(TB):
                    m = min(P, T - k * P)
                    last = te.transpose(tp[j][0:m, k * P:(k + 1) * P], key[name][:, k * P:k * P + m], ident[:, :])
                last.then_inc(product, 1)
            pe.wait_ge(setup_done, 1)

            for n, q in enumerate(passes):
                def after(name, cnt_, n=n):
                    pe.wait_ge(c[name].sem, item(name, n, cnt_))

                def sig(ins, name):
                    ins.then_inc(c[name].sem, 1)

                if q["kind"] == "node":
                    if not does_mm(q):
                        continue
                    def chunks(g, q=q, n=n):
                        for ch, s, _, i in before(g):
                            after("normed", ch + 1)
                            x = v[s % 2] if q["tanh"] else o2[s]
                            after("moved", ch - 1)
                            for k in range(K // 2):
                                last = te.transpose(tp[s % 2][:, k * P:(k + 1) * P],
                                                    x[:, 2 * k:2 * k + 2, :].rearrange("p k d -> p (k d)"), ident[:, :])
                            sig(last, "transposed")
                        for ch, s, _, i in before(g):
                            after("moved", ch + 1)
                            after("biased", ch - 1)
                            for k in range(K // 2):
                                last = te.matmul(mm[s % 2][:, k * P:(k + 1) * P], vT[s % 2][:, k * P:(k + 1) * P],
                                                 q["mat"][:, :], start=True, stop=True)
                            sig(last, "multiplied")

                    pairs(pe, 0, chunks)
                else:
                    ends_of = 1 if q["kind"] == "rel" else 2
                    def turn_pair(g, q=q, ends_of=ends_of):
                        if q["act"]:
                            after("activated", g.n + 1)
                        else:
                            pe.wait_ge(gathered[g.s].sem, gathered[g.s].at[n] + 16 * G * ends_of * (g.i + 1))
                        after("pair_moved", g.n)
                        x = X[g.s].rearrange("p k e d -> p (k e d)")
                        for k in range(G * ends_of // 2):
                            last = te.transpose(ps_pair[:, k * P:(k + 1) * P], x[:, k * P:(k + 1) * P], ident)
                        sig(last, "pair_transposed")
                        after("pair_transposed", g.n + 1)
                        pe.sem_inc(c["x_used"].sem, 1)

                    def hidden(g, q=q):
                        after("pair_moved", g.n + 1)
                        after("hid_summed", g.n)
                        for k in range(G):
                            last = te.matmul(ps_hid[:, k * D:(k + 1) * D], XT[:, k * P:(k + 1) * P], we[q["layer"]],
                                             start=True, stop=True)
                        sig(last, "hid_ready")

                    def hidden_turned(g):
                        after("pair_moved", g.n + 1)
                        after("hid_moved", g.n)
                        sig(te.matmul(ps_hidT, piw1, XT, start=True, stop=True), "hid_ready")

                    def make_terms(g, q=q):
                        after("pair_moved" if q["kind"] == "rel" else "hid_moved", g.n + 1)
                        mat = q["mat"].rearrange("p r d -> p (r d)")
                        for h in range(2):
                            after("weighted", 2 * g.n - 1 + h)
                            for j in range(2):
                                if q["kind"] == "rel":
                                    x, w = XT[h * D:(h + 1) * D, j * P:(j + 1) * P], mat[h * D:(h + 1) * D, :]
                                else:
                                    x, w = hidT[:, (2 * j + h) * P:(2 * j + h + 1) * P], mat
                                last = te.matmul(ps_terms[q["terms"]][:, h, j, :], x, w, start=True, stop=True)
                            sig(last, "terms_ready")

                    def add_up(g):
                        after("parts_made", g.n + 1)
                        after("compared", g.n + 1)
                        after("sum_moved", g.n)
                        for t in range(G):
                            for k in range(G):
                                last = te.matmul(ps_parts[:, t, :], same_b[g.s][:, k, t * P:(t + 1) * P],
                                                 parts[g.s][:, k, :, :].rearrange("p c d -> p (c d)"),
                                                 start=(k == 0), stop=(k == G - 1))
                        sig(last, "sum_ready")

                    def add_up_turned(g):
                        after("msg_moved", g.n + 1)
                        after("compared", g.n + 1)
                        after("sumT_moved", g.n)
                        for k in range(G):
                            last = te.matmul(ps_sumT, msg[:, k, :], same[g.s][:, k, :],
                                             start=(k == 0), stop=(k == G - 1))
                        sig(last, "sumT_ready")

                    def project(g, q=q):
                        after("sumT_moved", g.n + 1)
                        after("sum_moved", g.n)
                        for k in range(G):
                            last = te.matmul(ps_sum[:, k * D:(k + 1) * D], sumT[:, k * P:(k + 1) * P],
                                             wnb[q["layer"]], start=True, stop=True)
                        sig(last, "sum_ready")

                    def rel(g):
                        dense_part(g)
                        if behind(g, 3):
                            add_up(behind(g, 3))
                        if behind(g, 0):
                            turn_pair(g)
                            make_terms(g)

                    def pair(g):
                        if behind(g, 3):
                            add_up(behind(g, 3))
                        if behind(g, 0):
                            turn_pair(g)
                        if behind(g, 1):
                            make_terms(behind(g, 1))
                        if behind(g, 0):
                            hidden_turned(g)

                    def mlp(g):
                        if behind(g, 0):
                            turn_pair(g)
                        dense_part(g)
                        if behind(g, 0):
                            hidden(g)
                        if behind(g, 1):
                            add_up_turned(behind(g, 1))
                        if behind(g, 1):
                            project(behind(g, 1))

                    def dense_multiply(h, q=q):
                        after("dense_moved", h.n + 1)
                        after("dense_done", h.n)
                        for k in range(HK // 2):
                            last = te.matmul(ps_dense[kind][:, k * P:(k + 1) * P],
                                             dense_xT[h.s][:, k * P:(k + 1) * P], q["dense"]["mat"],
                                             start=True, stop=True)
                        sig(last, "dense_made")

                    def dense_turn(h, q=q):
                        if q["dense"]["leaky"]:
                            after("dense_activated", h.n + 1)
                        else:
                            pe.wait_ge(dense_in[h.s].sem, dense_in[h.s].at[n] + 16 * (h.i + 1))
                        after("dense_moved", h.n)
                        for k in range(HK // 2):
                            last = te.transpose(ps_dense_T[kind][:, k * P:(k + 1) * P],
                                                dense_x[h.s][:, 2 * k:2 * k + 2, :].rearrange("p k d -> p (k d)"), ident)
                        sig(last, "dense_turned")

                    def dense_part(g, q=q):
                        if q["dense"] and behind(g, 3):
                            dense_multiply(behind(g, 3))
                        if q["dense"] and behind(g, 2):
                            dense_turn(behind(g, 2))

                    kind, do = q["kind"], {"rel": rel, "pair": pair, "mlp": mlp}
                    steps(pe, 3 if q["dense"] or kind != "mlp" else 1, do[kind])


_INS = ["x", "src", "dst", "edge_attr_8", "edge_type_8", "edge_weight",
        "L0_gnn_basis1", "L0_gnn_coeff1", "L0_gnn_loop_w1", "L0_gnn_bias1",
        "L0_gnn_basis2", "L0_gnn_coeff2", "L0_gnn_loop_w2", "L0_gnn_bias2",
        "L1_gnn_pp_W", "L1_gnn_pp_b", "L1_gnn_pi_W1", "L1_gnn_pi_b1", "L1_gnn_pi_W2", "L1_gnn_ii_W", "L1_gnn_ii_b",
        "L2_gnn_We0", "L2_gnn_be0", "L2_gnn_Wn0", "L2_gnn_bn0", "L2_gnn_We1", "L2_gnn_be1", "L2_gnn_Wn1",
        "L2_gnn_bn1", "L2_gnn_We2", "L2_gnn_be2", "L2_gnn_Wn2", "L2_gnn_bn2", "L3_gnn_W"]


def kernel(**inputs):
    import numpy as np
    import concourse.bacc as bacc
    from concourse.bass_utils import run_bass_kernel_spmd as run

    nc = bacc.Bacc("TRN2", target_bir_lowering=False, num_devices=1)
    arrays, aps = {}, {}
    for name in _INS:
        v = np.ascontiguousarray(inputs[name])
        arrays["in_" + name] = v
        aps[name] = nc.dram_tensor("in_" + name, v.shape, mybir.dt.from_np(v.dtype), kind="ExternalInput").ap()
    shape = inputs["x"].shape
    out = nc.dram_tensor("out_x", shape, mybir.dt.float32, kind="ExternalOutput").ap()
    build(nc, aps, out)
    return run(nc, [arrays], core_ids=[0]).results[0]["out_x"]
```
